# Optimizing a Trainium2 kernel written in Bass

```python
import numpy as np
import jax
import jax.numpy as jnp

def _softmax(x, axis=-1):
    return jax.nn.softmax(x, axis=axis)

def _gelu(x):
    return jax.nn.gelu(x, approximate=True)

def _silu(x):
    return jax.nn.silu(x)

def _sigmoid(x):
    return jax.nn.sigmoid(x)

def _layernorm(x, axis=-1, eps=1e-05):
    m = jnp.mean(x, axis=axis, keepdims=True)
    v = jnp.var(x, axis=axis, keepdims=True)
    return (x - m) / jnp.sqrt(v + eps)

def _scatter_add(tgt, idx, src, axis=0):
    return tgt.at[idx].add(src)

def _segment_sum(src, seg, n):
    return jax.ops.segment_sum(src, seg, n)
kernel_name = 'mk_seq_preln_d1_jaxref_r4_01d07f'

def setup_inputs(seed: int=0):
    np.random.seed(seed)
    _w = jnp.asarray

    def _L0_attn_setup():
        import jax, jax.numpy as jnp
        import numpy as np
        D_MODEL, D_STATE, D_INNER = (256, 8, int(256 * 1.5))
        LN_EPS = 1e-05

        def layer_norm(x, g, b):
            mu = jnp.mean(x, axis=-1, keepdims=True)
            var = jnp.mean(jnp.square(x - mu), axis=-1, keepdims=True)
            return (x - mu) / jnp.sqrt(var + LN_EPS) * g + b
        key = jax.random.key(seed)
        ks = jax.random.split(key, 8)
        x = jax.random.normal(ks[0], (4, 512, D_MODEL), dtype=jnp.float32)
        W_in = jax.random.normal(ks[1], (2 * D_INNER, D_MODEL), dtype=jnp.float32) * 0.02
        W_out = jax.random.normal(ks[2], (D_MODEL, D_INNER), dtype=jnp.float32) * 0.02
        A_init = jax.random.normal(ks[3], (D_INNER, D_STATE), dtype=jnp.float32) * 0.1
        A_log = jnp.log(jnp.abs(A_init) + 0.1)
        B = jax.random.normal(ks[4], (D_INNER, D_STATE), dtype=jnp.float32) * 0.1
        C = jax.random.normal(ks[5], (D_INNER, D_STATE), dtype=jnp.float32) * 0.01
        ln_in_g = jnp.ones((D_MODEL,), jnp.float32)
        ln_in_b = jnp.zeros((D_MODEL,), jnp.float32)
        ln_out_g = jnp.ones((D_MODEL,), jnp.float32)
        ln_out_b = jnp.zeros((D_MODEL,), jnp.float32)
        return {'x': x, 'W_in': W_in, 'W_out': W_out, 'A_log': A_log, 'B': B, 'C': C, 'ln_in_g': ln_in_g, 'ln_in_b': ln_in_b, 'ln_out_g': ln_out_g, 'ln_out_b': ln_out_b}
    _L0_attn_in = _L0_attn_setup()

    def _L0_ffn_setup():
        import jax, jax.numpy as jnp
        import numpy as np
        HIDDEN = 256
        INTER = 512
        NUM_EXPERTS = 8
        TOPK = 2
        STD = 0.02
        key = jax.random.key(seed)
        k1, k2, k3, k4 = jax.random.split(key, 4)
        return {'hidden_states': jax.random.normal(k1, (1, 512, HIDDEN), dtype=jnp.float32), 'w1': jax.random.normal(k2, (NUM_EXPERTS, 2 * INTER, HIDDEN), dtype=jnp.float32) * STD, 'w2': jax.random.normal(k3, (NUM_EXPERTS, HIDDEN, INTER), dtype=jnp.float32) * STD, 'router_w': jax.random.normal(k4, (NUM_EXPERTS, HIDDEN), dtype=jnp.float32) * STD}
    _L0_ffn_in = _L0_ffn_setup()
    _d = {'L0_attn_x': _L0_attn_in['x'], 'L0_attn_W_in': _L0_attn_in['W_in'], 'L0_attn_W_out': _L0_attn_in['W_out'], 'L0_attn_A_log': _L0_attn_in['A_log'], 'L0_attn_B': _L0_attn_in['B'], 'L0_attn_C': _L0_attn_in['C'], 'L0_attn_ln_in_g': _L0_attn_in['ln_in_g'], 'L0_attn_ln_in_b': _L0_attn_in['ln_in_b'], 'L0_attn_ln_out_g': _L0_attn_in['ln_out_g'], 'L0_attn_ln_out_b': _L0_attn_in['ln_out_b'], 'L0_ffn_w1': _L0_ffn_in['w1'], 'L0_ffn_w2': _L0_ffn_in['w2'], 'L0_ffn_router_w': _L0_ffn_in['router_w']}
    _x0 = _d['L0_attn_x']
    _d['L0_attn_x'] = jax.random.normal(jax.random.fold_in(jax.random.key(seed), 1), (16, 512, 256), dtype=_x0.dtype)
    del _x0
    return _d

def reference(L0_attn_x, L0_attn_W_in, L0_attn_W_out, L0_attn_A_log, L0_attn_B, L0_attn_C, L0_attn_ln_in_g, L0_attn_ln_in_b, L0_attn_ln_out_g, L0_attn_ln_out_b, L0_ffn_w1, L0_ffn_w2, L0_ffn_router_w):

    def _L0_attn_ref(x, W_in, W_out, A_log, B, C, ln_in_g, ln_in_b, ln_out_g, ln_out_b):
        import jax, jax.numpy as jnp
        import numpy as np
        D_MODEL, D_STATE, D_INNER = (256, 8, int(256 * 1.5))
        LN_EPS = 1e-05

        def layer_norm(x, g, b):
            mu = jnp.mean(x, axis=-1, keepdims=True)
            var = jnp.mean(jnp.square(x - mu), axis=-1, keepdims=True)
            return (x - mu) / jnp.sqrt(var + LN_EPS) * g + b
        Bb, L, D = x.shape
        x_norm = layer_norm(x, ln_in_g, ln_in_b)
        x_proj = jnp.clip(x_norm @ W_in.T, -5.0, 5.0)
        x_ssm, gate = jnp.split(x_proj, 2, axis=-1)
        A = jnp.clip(-jnp.exp(jnp.clip(A_log, -5.0, 0.0)), -2.0, -0.01)
        decay = A * 0.9

        def step(h, x_t):
            h = h * decay + x_t[:, :, None] * B[None] * 0.1
            h = jnp.clip(h, -5.0, 5.0)
            y = jnp.clip(jnp.einsum('bid,id->bi', h, C), -5.0, 5.0)
            return (h, y)
        h0 = jnp.zeros((Bb, D_INNER, D_STATE), x.dtype)
        _, ys = jax.lax.scan(step, h0, jnp.swapaxes(x_ssm, 0, 1))
        out_ssm = jnp.swapaxes(ys, 0, 1)
        out = out_ssm * jnp.tanh(gate) @ W_out.T
        out = jnp.clip(out, -5.0, 5.0)
        return layer_norm(out, ln_out_g, ln_out_b)

    def _L0_ffn_ref(hidden_states, w1, w2, router_w):
        import jax, jax.numpy as jnp
        import numpy as np
        HIDDEN = 256
        INTER = 512
        NUM_EXPERTS = 8
        TOPK = 2
        STD = 0.02
        orig_shape = hidden_states.shape
        dtype = hidden_states.dtype
        x = hidden_states.reshape(-1, orig_shape[-1])
        E = w1.shape[0]
        gating = x @ router_w.T
        probs = jax.nn.softmax(gating.astype(jnp.float32), axis=-1)
        topk_w, sel = jax.lax.top_k(probs, TOPK)
        topk_w = topk_w.astype(dtype)
        combine = (jax.nn.one_hot(sel, E, dtype=dtype) * topk_w[..., None]).sum(axis=1)
        h = jnp.einsum('td,eid->tei', x, w1)
        gate = jax.nn.silu(h[..., :INTER])
        y = h[..., INTER:] * gate
        out = jnp.einsum('tei,ehi,te->th', y, w2, combine)
        return out.reshape(orig_shape)
    x = L0_attn_x
    x = x + _L0_attn_ref(_layernorm(x, axis=-1), L0_attn_W_in, L0_attn_W_out, L0_attn_A_log, L0_attn_B, L0_attn_C, L0_attn_ln_in_g, L0_attn_ln_in_b, L0_attn_ln_out_g, L0_attn_ln_out_b)
    x = x + _L0_ffn_ref(_layernorm(x, axis=-1), L0_ffn_w1, L0_ffn_w2, L0_ffn_router_w)
    return x

_drawn_inputs = setup_inputs


def setup_inputs(seed=0):
    import zlib

    import numpy as np

    out = dict(_drawn_inputs(seed))
    spreads = {'L0_attn_ln_in_g': (1.0, 0.6),
     'L0_attn_ln_in_b': (0.0, 0.8),
     'L0_attn_ln_out_g': (1.0, 0.6),
     'L0_attn_ln_out_b': (0.0, 0.1)}
    factors = {'L0_attn_W_in': 8.0,
     'L0_attn_W_out': 8.0,
     'L0_attn_A_log': 8.0,
     'L0_attn_B': 8.0,
     'L0_attn_C': 8.0,
     'L0_ffn_w1': 8.0,
     'L0_ffn_w2': 8.0,
     'L0_ffn_router_w': 8.0}
    for name, (base, spread) in spreads.items():
        noise = np.random.default_rng([zlib.crc32(name.encode()), seed]).standard_normal(out[name].shape)
        drawn = base * np.exp(spread * noise) if base else spread * noise
        out[name] = jnp.asarray(drawn.astype(out[name].dtype))
    for name, factor in factors.items():
        out[name] = (out[name] * factor).astype(out[name].dtype)
    return out
```

```python
from contextlib import ExitStack

import concourse.bass as bass
from concourse import mybir

F32 = mybir.dt.float32
BF16 = mybir.dt.bfloat16
I32 = mybir.dt.int32
U32 = mybir.dt.uint32
ALU = mybir.AluOpType
ACT = mybir.ActivationFunctionType
AX_X = mybir.AxisListType.X

P = 128
LN_EPS = 1e-5
CLIP = 5.0
TANH_CLIP = 0.9999092042625951
PAD_TOKEN = 1 << 20


def lagged(m, u, d, count, n=2):
    if isinstance(m, int) and not 0 <= n * m + u - d < count:
        return None
    return n * m + (u - d), (u - d) % n, m + (u - d) // n


def first(b, n):
    return isinstance(b, int) and b < n


def wait_apart(eng, held, met, *waits):
    ready = []
    for n, (sem, value) in enumerate(waits):
        if not isinstance(value, int):
            at = held.get((eng.engine, n)) or held.setdefault((eng.engine, n), eng.alloc_register(f"apart{n}"))
            eng.reg_mov(at, value)
            value = at
        ready.append((sem, value))
    eng.wait_ge(*met)
    for sem, value in ready:
        eng.wait_ge(sem, value)


class Chain:

    def __init__(self, eng, sem, per):
        self.eng, self.sem, self.per = eng, sem, per

    def begin(self, b):
        self.b, self.k = b, 0

    def link(self, ins):
        ins.then_inc(self.sem, 1)
        self.k += 1
        assert self.k <= self.per

    def wait(self):
        if not first(self.b, 1) or self.k:
            self.eng.wait_ge(self.sem, self.per * self.b + self.k)

    def step(self, ins):
        self.link(ins)
        self.wait()

    def wait_apart(self, held, met):
        wait_apart(self.eng, held, met, (self.sem, self.per * self.b + self.k))

    def end(self):
        assert self.k == self.per, (self.k, self.per)


def build(nc, x, w_in_t, w_out_t, a_log, b_in, c_out, g_in, bias_in, g_out, bias_out,
          w1_t, w2_t, router_t, out):
    NB, L, D = x.shape
    CT = L // P
    KD = D // P
    DI = w_in_t.shape[1] // 2
    NC = DI // P
    NS = a_log.shape[1]
    E, _, I2 = w1_t.shape
    I = I2 // 2
    KI = I // P
    T = NB * L
    TOP = 2
    NT = T * TOP // P + E - 1
    REGION = T
    ROWS = E * REGION + P * E

    x_v = x.rearrange("b (c p) d -> b p c d", p=P)
    out_v = out.rearrange("b (c p) d -> b p c d", p=P)
    out_rows = out.rearrange("b l d -> (b l) d")
    r_rows = nc.dram_tensor("expert_input_rows", [T, D], F32).ap()
    r_v = r_rows.rearrange("(b c p) d -> b p c d", p=P, c=CT)
    table = nc.dram_tensor("slot_table", [ROWS, 2], I32).ap()

    with ExitStack() as ctx:
        def sb(name, shape, dt=F32):
            return ctx.enter_context(nc.sbuf_tensor(name, shape, dt))

        def psum(name):
            return ctx.enter_context(nc.psum_tensor(name, [P, 512], F32))

        def sem(name):
            return ctx.enter_context(nc.semaphore(name))

        w1 = sb("w1", [P, KD, E * I2])
        w2 = sb("w2", [P, KI, E * D])
        wi = sb("wi", [P, KD, 2 * DI])
        wo = sb("wo", [P, NC, D])
        rw = sb("rw", [P, KD, E])
        gout = sb("gout", [P, D])
        bout = sb("bout", [P, D])
        gin = sb("gin", [P, KD])
        bin_ = sb("bin", [P, KD])
        ident = sb("ident", [P, P])
        upper = sb("upper", [P, P], BF16)
        onesb = sb("onesb", [P, P], BF16)
        ones1 = sb("ones1", [P, 1])
        mhalf = sb("mhalf", [P, CT])
        iota8 = sb("iota8", [P, E])
        ids = sb("ids", [P, CT])
        alog = sb("alog", [P, NC, NS])
        bmat = sb("bmat", [P, NC, NS])
        cmat = sb("cmat", [P, NC, NS])
        dec = sb("dec", [P, NC, NS])
        ssm_t = sb("ssm_t", [P, NC, NS])
        ssm_u = sb("ssm_u", [P, NC, NS])
        wsum = sb("wsum", [P, NC])
        viol = sb("viol", [P, 1])
        general = sb("general", [1, 1], I32)
        pbias = sb("pbias", [P, 2 * NC])
        decay_row = sb("decay_row", [P, NC, L])
        x_in = [sb(f"x_in{i}", [P, CT, D]) for i in range(2)]
        x_res = [sb(f"x_res{i}", [P, CT, D]) for i in range(2)]
        xhat = sb("xhat", [P, CT, D])
        xhat_t = sb("xhat_t", [P, KD, L])
        xs = [sb(f"xs{i}", [P, NC, L]) for i in range(2)]
        gate = [sb(f"gate{i}", [P, NC, L]) for i in range(2)]
        state = sb("state", [P, NC, L])
        o = sb("o", [P, CT, D])
        r = sb("r", [P, CT, D])
        r_t = sb("r_t", [P, KD, L])
        stats = sb("stats", [P, 3, CT, 6])
        mv = sb("mv", [P, 3, CT, 2])
        var = sb("var", [P, 3, CT])
        rstd = sb("rstd", [P, 3, CT])
        lg = sb("lg", [P, CT, E])
        mx = sb("mx", [P, CT])
        ex = sb("ex", [P, CT, E])
        den = sb("den", [P, CT])
        prob = sb("prob", [P, CT, E])
        top = sb("top", [P, CT, 8])
        top_i = sb("top_i", [P, CT, 8], U32)
        top_f = sb("top_f", [P, CT, TOP])
        hot = sb("hot", [P, TOP, CT, E])
        mask = sb("mask", [P, CT, E], BF16)
        before = sb("before", [P, CT + 1, E], BF16)
        slot_f = sb("slot_f", [P, CT, E])
        pick = sb("pick", [P, TOP, CT, E])
        slot_sum = sb("slot_sum", [P, TOP, CT])
        slot = [sb(f"slot{i}", [P, TOP, CT], U32) for i in range(2)]
        row = [sb(f"row{i}", [P, TOP, CT, 2], I32) for i in range(2)]
        cnt = sb("cnt", [P, E])
        n_e = sb("n_e", [1, E])
        step128 = sb("step128", [1, T // P])
        cmp_t = x_in[0][0:1, 0:2, :].rearrange("p c d -> p (c d)").rearrange("p (e n) -> p e n", e=E)
        tiles_e = sb("tiles_e", [1, E])
        ones8 = sb("ones8", [1, E])
        incl = sb("incl", [1, E])
        tile_no = sb("tile_no", [1, NT])
        past, past_t = (x_in[i][0:1, :, :].rearrange("p c d -> p (c d)")[:, 0:NT * (E - 1)]
                        .rearrange("p (n e) -> p n e", e=E - 1) for i in range(2))
        e_of = sb("e_of", [1, NT])
        start_of = sb("start_of", [1, NT])
        row_f = sb("row_f", [1, NT])
        tile_e = sb("tile_e", [1, NT], I32)
        tile_row = sb("tile_row", [1, NT], I32)
        tb = [sb(f"tb{i}", [P, 2], I32) for i in range(4)]
        xg_t = [xs[i][:, 0, 0:D].rearrange("p (k q) -> p k q", k=KD) for i in range(2)]
        act_s = [xs[i][:, 1, 0:I] for i in range(2)]
        act_y = [xs[i][:, 2, 0:I] for i in range(2)]
        y_t = [gate[i][:, 0, 0:I].rearrange("p (k q) -> p k q", k=KI) for i in range(2)]
        xg = [state[:, i, 0:D] for i in range(2)]
        y_out = [state[:, i, D:2 * D] for i in range(2)]
        pad_src = w1[:, 0, 0:ROWS // P * 2].bitcast(I32)

        PT = [psum("PT0"), psum("PT1")]
        PG = [psum("PG0"), psum("PG1")]
        PO = [psum("PO0"), psum("PO1")]
        PR = psum("PR")
        PM = psum("PM")
        m_logit = PM[:, 0:CT * E].rearrange("p (c e) -> p c e", e=E)
        m_rank = PM[:, 64:64 + (CT + 1) * E].rearrange("p (c e) -> p c e", e=E)
        m_bias = PM[:, 128:128 + 2 * NC]
        m_viol = PM[0:1, 140:141]

        s_const = sem("s_const")
        s_wload = sem("s_wload")
        s_x = [sem(f"s_x{i}") for i in range(2)]
        s_xr = [sem(f"s_xr{i}") for i in range(2)]
        s_out = [sem(f"s_out{i}") for i in range(2)]
        s_padset = sem("s_padset")
        s_pad = sem("s_pad")
        s_pool0 = sem("s_pool0")
        s_setup = sem("s_setup")
        s_exp0 = sem("s_exp0")
        s_bias_mm = sem("s_bias_mm")
        s_ready = sem("s_ready")
        s_biascopy = sem("s_biascopy")
        s_flag = sem("s_flag")
        s_a_dve = sem("s_a_dve")
        s_a_var = sem("s_a_var")
        s_a_rstd = sem("s_a_rstd")
        s_xhat = sem("s_xhat")
        s_tx = sem("s_tx")
        s_txc = sem("s_txc")
        s_proj = sem("s_proj")
        s_projc = sem("s_projc")
        s_b_dve = sem("s_b_dve")
        s_z = sem("s_z")
        s_omm = sem("s_omm")
        s_o = sem("s_o")
        s_c_dve = sem("s_c_dve")
        s_c_var = sem("s_c_var")
        s_c_rstd = sem("s_c_rstd")
        s_resb = sem("s_resb")
        s_xnew = sem("s_xnew")
        s_r = sem("s_r")
        s_d_dve = sem("s_d_dve")
        s_s_dve = sem("s_s_dve")
        s_tr = sem("s_tr")
        s_trc = sem("s_trc")
        s_logit = sem("s_logit")
        s_lg = sem("s_lg")
        s_ex = sem("s_ex")
        s_mask = sem("s_mask")
        s_rank = sem("s_rank")
        s_rankread = sem("s_rankread")
        s_slot = sem("s_slot")
        s_rows = [sem(f"s_rows{i}") for i in range(2)]
        s_tiles = sem("s_tiles")
        s_tile_tab = sem("s_tile_tab")
        s_tb = [sem(f"s_tb{i}") for i in range(4)]
        s_xgset = sem("s_xgset")
        s_xg = [sem(f"s_xg{i}") for i in range(2)]
        s_gt = sem("s_gt")
        s_gtc = sem("s_gtc")
        s_h = sem("s_h")
        s_silu = sem("s_silu")
        s_y = sem("s_y")
        s_yt = sem("s_yt")
        s_ytc = sem("s_ytc")
        s_mo = sem("s_mo")
        s_yout = sem("s_yout")
        s_add = [sem(f"s_add{i}") for i in range(2)]

        held = {}
        block = ctx.enter_context(nc.Block())

        PEEL, LAGS = 4, 4

        def batches(eng, step):
            for s in range(PEEL):
                step(s // 2, s % 2)
            with eng.Fori(PEEL // 2, NB // 2) as m:
                for u in range(2):
                    step(m, u)
            for s in range(NB, NB + LAGS):
                step(s // 2, s % 2)

        U = 4

        def tiles(eng, step, ahead=0):
            last = NT // U - (1 if ahead else 0)
            for s in range(U):
                step(0, s)
            with eng.Fori(1, last) as m:
                for u in range(U):
                    step(m, u)
            for s in range(U * last, NT + 1):
                step(s // U, s % U)

        def tile(m, u, d):
            at = lagged(m, u, d, NT, U)
            return at and (at[0], at[1] % 2, at[2] * (U // 2) + at[1] // 2, at[1], at[2])

        N_CONST = 12

        @block.sync
        def _(sp):
            def load_x(at):
                b, par, half = at
                if not first(b, 2):
                    sp.wait_ge(s_xhat, CT * (b - 1))
                sp.dma_start(x_in[par][:, :, :], x_v[b]).then_inc(s_x[par], 16)

            load_x((0, 0, 0))
            for dst, src in ((wi[:, :, :], w_in_t.rearrange("(k p) n -> p k n", p=P)),
                             (gin[:, :], g_in),
                             (bin_[:, :], bias_in),
                             (alog[:, :, :], a_log.rearrange("(c p) d -> p c d", p=P)),
                             (bmat[:, :, :], b_in.rearrange("(c p) d -> p c d", p=P)),
                             (cmat[:, :, :], c_out.rearrange("(c p) d -> p c d", p=P)),
                             (wo[:, :, :], w_out_t.rearrange("(c p) n -> p c n", p=P)),
                             (rw[:, :, :], router_t.rearrange("(k p) e -> p k e", p=P)),
                             (gout[:, :], g_out.partition_broadcast(P)),
                             (bout[:, :], bias_out.partition_broadcast(P))):
                sp.dma_start(dst, src).then_inc(s_const, 16)
            load_x((1, 1, 0))
            sp.wait_ge(s_padset, 1)
            sp.dma_start(table.rearrange("(p n) t -> p (n t)", p=P), pad_src).then_inc(s_pad, 16)
            sp.wait_ge(s_pad, 16)
            for e in range(E):
                sp.dma_start(w1[:, :, e * I2:(e + 1) * I2],
                             w1_t[e].rearrange("(k p) n -> p k n", p=P)).then_inc(s_wload, 16)
                sp.dma_start(w2[:, :, e * D:(e + 1) * D],
                             w2_t[e].rearrange("(k p) n -> p k n", p=P)).then_inc(s_wload, 16)

            def step(m, u):
                nxt = lagged(m, u, -2, NB)
                if nxt:
                    load_x(nxt)
                at = lagged(m, u, 1, NB)
                if at:
                    b, par, half = at
                    if not first(b, 2):
                        sp.wait_ge(s_out[par], 32 * half)
                    sp.dma_start(x_res[par][:, :, :], x_v[b]).then_inc(s_xr[par], 16)
                at = lagged(m, u, 2, NB)
                if at:
                    b, par, half = at
                    sp.wait_ge(s_xnew, CT * (b + 1))
                    sp.dma_start(out_v[b], x_res[par][:, :, :]).then_inc(s_out[par], 16)
                    sp.wait_ge(s_r, CT * (b + 1))
                    sp.dma_start(r_v[b], r[:, :, :]).then_inc(s_out[par], 16)

            for s in range(PEEL):
                step(s // 2, s % 2)
            with sp.Fori(PEEL // 2, NB // 2 - 1) as m:
                for u in range(2):
                    step(m, u)
            for s in range(NB - 2, NB + LAGS):
                step(s // 2, s % 2)

            sp.wait_ge(s_tiles, 2)
            for i in range(2):
                sp.wait_ge(s_rows[i], 16 * TOP * CT * NB // 2)

            def load_rows(j, i, uses):
                if not first(j, 4):
                    sp.wait_ge(s_add[i % 2], 16 * (2 * uses - 1 if i < 2 else 2 * uses))
                at = sp.value_load(tile_row[0:1, bass.ds(j, 1)], min_val=0, max_val=ROWS - P)
                sp.dma_start(tb[i][:, :], table[bass.ds(at, P), :]).then_inc(s_tb[i], 16)

            for j in range(4):
                load_rows(j, j, 0)
            with sp.Fori(1, NT // 4) as q:
                for i in range(4):
                    load_rows(4 * q + i, i, q)
            for j in range(NT // 4 * 4, NT):
                load_rows(j, j % 4, j // 4)
            for i in range(2):
                sp.wait_ge(s_add[i], 16 * ((NT + 1 - i) // 2))

        @block.gpsimd
        def _(pool):
            for n, (t, v) in enumerate(((ident, 0.0), (upper, 0.0), (onesb, 1.0), (ones1, 1.0), (mhalf, -0.5),
                                        (decay_row, 1.0), (ones8, 1.0))):
                pool.memset(t[:], v).then_inc(s_pool0, 1)
            pool.memset(pad_src, 0).then_inc(s_pool0, 1)
            pool.memset(before[:], 0.0).then_inc(s_pool0, 1)
            pool.wait_ge(s_pool0, 9)
            pool.affine_select(out=ident[:], in_=ident[:], compare_op=ALU.not_equal, fill=1.0,
                               base=0, pattern=[[-1, P]], channel_multiplier=1).then_inc(s_pool0, 1)
            pool.affine_select(out=upper[:], in_=upper[:], compare_op=ALU.is_ge, fill=1.0,
                               base=0, pattern=[[-1, P]], channel_multiplier=1).then_inc(s_pool0, 1)
            pool.memset(pad_src.rearrange("p (n t) -> p n t", t=2)[:, :, 0], PAD_TOKEN).then_inc(s_padset, 1)
            pool.iota(iota8[:], pattern=[[1, E]], base=0, channel_multiplier=0,
                      allow_small_or_imprecise_dtypes=True).then_inc(s_pool0, 1)
            pool.iota(ids[:], pattern=[[P, CT]], base=0, channel_multiplier=1,
                      allow_small_or_imprecise_dtypes=True).then_inc(s_pool0, 1)
            pool.iota(cnt[:], pattern=[[REGION, E]], base=0, channel_multiplier=0,
                      allow_small_or_imprecise_dtypes=True).then_inc(s_pool0, 1)
            pool.iota(step128[:], pattern=[[P, T // P]], base=0, channel_multiplier=0,
                      allow_small_or_imprecise_dtypes=True).then_inc(s_pool0, 1)
            pool.iota(tile_no[:], pattern=[[1, NT]], base=0, channel_multiplier=0,
                      allow_small_or_imprecise_dtypes=True).then_inc(s_pool0, 1)
            pool.wait_ge(s_const, 160)

            def scatter(at, first_k, count):
                b, par, half = at
                for n in range(first_k, first_k + count):
                    k, c = divmod(n, CT)
                    pool.indirect_dma_start(
                        out=table, out_offset=bass.IndirectOffsetOnAxis(ap=slot[par][:, k, c:c + 1], axis=0),
                        in_=row[par][:, k, c, :], in_offset=None).then_inc(s_rows[par], 16)

            def step(m, u):
                at_a, at_r, at_c, at_s = (lagged(m, u, n, NB) for n in (0, 1, 2, 4))
                if at_a:
                    pool.wait_ge(s_a_var, at_a[0] + 1)
                    pool.tensor_tensor(rstd[:, 0, :], var[:, 0, :], mhalf[:], ALU.pow).then_inc(s_a_rstd, 1)
                if at_r:
                    b, par, half = at_r
                    pool.wait_ge(s_xr[par], 16 * (half + 1))
                    for c in range(CT):
                        pool.tensor_tensor(x_res[par][:, c, :], x_res[par][:, c, :], bout[:],
                                           ALU.add).then_inc(s_resb, 1)
                if at_s:
                    wait_apart(pool, held, (s_pad, 16), (s_slot, at_s[0] + 1))
                    scatter(at_s, 0, 2)
                if at_c:
                    pool.wait_ge(s_c_var, 2 * at_c[0] + 1)
                    pool.tensor_tensor(rstd[:, 1, :], var[:, 1, :], mhalf[:], ALU.pow).then_inc(s_c_rstd, 1)
                if at_s:
                    scatter(at_s, 2, 3)
                if at_c:
                    pool.wait_ge(s_c_var, 2 * at_c[0] + 2)
                    pool.tensor_tensor(rstd[:, 2, :], var[:, 2, :], mhalf[:], ALU.pow).then_inc(s_c_rstd, 1)
                if at_s:
                    scatter(at_s, 5, 3)

            batches(pool, step)

            for i in range(2):
                pool.wait_ge(s_out[i], 32 * (NB // 2))
            for i in range(2):
                pool.memset(xg[i], 0.0).then_inc(s_xgset, 1)
            pool.wait_ge(s_xgset, 2)

            def gather(at):
                j, par, uses, i, tb_uses = at
                waits = [(s_tb[i], 16 * (tb_uses + 1))] + ([] if first(j, 2) else [(s_gt, j - 1)])
                wait_apart(pool, held, (s_pad, 16), *waits)
                pool.indirect_dma_start(
                    out=xg[par], out_offset=None, in_=r_rows,
                    in_offset=bass.IndirectOffsetOnAxis(ap=tb[i][:, 0:1].bitcast(U32), axis=0),
                    bounds_check=T - 1, oob_is_err=False).then_inc(s_xg[par], 16)

            def add(at):
                j, par, uses, i, tb_uses = at
                waits = [(s_yout, j + 1)] + ([] if first(j, 1) else [(s_add[1 - par], 16 * (uses + par))])
                wait_apart(pool, held, (s_pad, 16), *waits)
                pool.indirect_dma_start(
                    out=out_rows, out_offset=bass.IndirectOffsetOnAxis(ap=tb[i][:, 0:1].bitcast(U32), axis=0),
                    in_=y_out[par], in_offset=None,
                    bounds_check=T - 1, oob_is_err=False, compute_op=ALU.add).then_inc(s_add[par], 16)

            def tile_step(m, u):
                if at := tile(m, u, -2):
                    gather(at)
                if at := tile(m, u, 1):
                    add(at)

            for j in range(2):
                gather(tile(0, j, 0))
            tiles(pool, tile_step, ahead=2)

        @block.scalar
        def _(act):
            act.wait_ge(s_setup, 1)
            act.activation(ssm_u[:, :, :], ssm_t[:, :, :], ACT.Exp).then_inc(s_exp0, 1)
            act.wait_ge(s_bias_mm, 1)
            act.copy(pbias[:], m_bias).then_inc(s_biascopy, 1)
            act.wait_ge(s_biascopy, 1)

            def step(m, u):
                if at := lagged(m, u, 3, NB):
                    b, par, half = at
                    for k in range(KD):
                        act.wait_ge(s_tr, KD * b + k + 1)
                        act.copy(r_t[:, k, :], PR[:, :]).then_inc(s_trc, 1)
                if at := lagged(m, u, 0, NB):
                    b, par, half = at
                    for k in range(KD):
                        act.wait_ge(s_tx, KD * b + k + 1)
                        act.copy(xhat_t[:, k, :], PT[k][:, :]).then_inc(s_txc, 1)
                if at := lagged(m, u, 3, NB):
                    b, par, half = at
                    act.wait_ge(s_lg, b + 1)
                    act.activation(ex[:, :, :], lg[:, :, :], ACT.Exp).then_inc(s_ex, 1)
                if at := lagged(m, u, 0, NB):
                    b, par, half = at
                    for j in range(2 * NC):
                        act.wait_ge(s_proj, 2 * NC * b + j + 1)
                        dst = xs[par] if j < NC else gate[par]
                        act.activation(dst[:, j % NC, :], PG[j % 2][:, :], ACT.Identity if j < NC else ACT.Tanh,
                                       bias=pbias[:, j:j + 1]).then_inc(s_projc, 1)

            batches(act, step)

            def copy_gathered(at):
                j, par, _, _, _ = at
                act.wait_ge(s_gt, j + 1)
                act.copy(xg_t[par], PR[:, 0:D].rearrange("p (k q) -> p k q", k=KD)).then_inc(s_gtc, 1)

            def tile_step(m, u):
                now, last, nxt = (tile(m, u, n) for n in (0, 1, -1))
                if last:
                    j, par, uses, i, tb_uses = last
                    act.wait_ge(s_yt, j + 1)
                    act.copy(y_t[par], PO[1][:, :].rearrange("p (k q) -> p k q", k=KI)).then_inc(s_ytc, 1)
                if now:
                    j, par, _, _, _ = now
                    act.wait_ge(s_h, j + 1)
                    act.activation(act_s[par], [PT, PG][par][0][:, :], ACT.Silu).then_inc(s_silu, 1)
                if nxt:
                    copy_gathered(nxt)
                if last:
                    j, par, uses, i, tb_uses = last
                    act.wait_ge(s_mo, j + 1)
                    if not first(j, 2):
                        act.wait_ge(s_add[par], 16 * uses)
                    act.wait_ge(s_tb[i], 16 * (tb_uses + 1))
                    act.activation(y_out[par], PO[0][:, 0:D], ACT.Copy,
                                   scale=tb[i][:, 1:2].bitcast(F32)).then_inc(s_yout, 1)

            copy_gathered(tile(0, 0, 0))
            tiles(act, tile_step, ahead=1)

        @block.vector
        def _(dve):
            setup = Chain(dve, s_setup, 15)
            setup.begin(0)
            dve.wait_ge(s_const, 160)
            setup.step(dve.tensor_scalar(ssm_t[:], alog[:], -5.0, 0.0, ALU.max, ALU.min))
            dve.wait_ge(s_exp0, 1)
            setup.step(dve.tensor_scalar(dec[:], ssm_u[:], -1.0, -2.0, ALU.mult, ALU.max))
            setup.step(dve.tensor_scalar(dec[:], dec[:], -0.01, 0.9, ALU.min, ALU.mult))
            setup.step(dve.tensor_tensor(ssm_t[:], bmat[:], cmat[:], ALU.mult))
            setup.step(dve.tensor_reduce(wsum[:], ssm_t[:], AX_X, ALU.add))
            setup.step(dve.tensor_scalar(wsum[:], wsum[:], 0.1, None, ALU.mult))
            dve.wait_ge(s_pool0, 16)
            for c in range(NC):
                ins = dve.tensor_scalar(decay_row[:, c, :], decay_row[:, c, :], dec[:, c, 0:1], None, ALU.mult)
            setup.step(ins)
            setup.step(dve.scalar_tensor_tensor(out=ssm_t[:], in0=bmat[:], scalar=-1.0, in1=bmat[:],
                                                op0=ALU.mult, op1=ALU.max))
            setup.step(dve.tensor_scalar(ssm_u[:], dec[:], 9.998, 9.998, ALU.mult, ALU.add))
            setup.step(dve.tensor_tensor(ssm_t[:], ssm_t[:], ssm_u[:], ALU.is_gt))
            setup.step(dve.tensor_tensor(ssm_u[:], dec[:], dec[:, :, 0:1].to_broadcast([P, NC, NS]), ALU.not_equal))
            setup.step(dve.tensor_tensor(ssm_t[:], ssm_t[:], ssm_u[:], ALU.add))
            setup.step(dve.tensor_reduce(viol[:], ssm_t[:].rearrange("p c d -> p (c d)"), AX_X, ALU.add))
            dve.wait_ge(s_bias_mm, 1)
            for k in range(KD):
                setup.step(dve.tensor_scalar(wi[:, k, :], wi[:, k, :], gin[:, k:k + 1], None, ALU.mult))
            setup.end()
            dve.wait_ge(s_ready, 1)
            dve.tensor_copy(general[:], m_viol).then_inc(s_flag, 1)
            dve.wait_ge(s_flag, 1)
            is_general = dve.value_load(general[0:1, 0:1], min_val=0, max_val=1 << 20)

            ch_a = Chain(dve, s_a_dve, 2 * CT)
            ch_b = Chain(dve, s_b_dve, NC)
            ch_c = Chain(dve, s_c_dve, 5 * CT)
            ch_d = Chain(dve, s_d_dve, 6 + 3 * CT)
            ch_s = Chain(dve, s_s_dve, 4)

            def norm_stats(ch, n, src):
                for c in range(CT):
                    ch.link(dve.bn_stats(stats[:, n, c, :], src[:, c, :]))
                ch.wait_apart(held, (s_const, 160))
                for c in range(CT):
                    ch.link(dve.bn_aggr(mv[:, n, c, :], stats[:, n, c, :]))
                ch.wait()

            def stage_a(at):
                b, par, half = at
                ch_a.begin(b)
                ch_a.wait()
                dve.wait_ge(s_x[par], 16 * (half + 1))
                norm_stats(ch_a, 0, x_in[par])
                dve.tensor_scalar(var[:, 0, :], mv[:, 0, :, 1], 1.0 + LN_EPS, LN_EPS * LN_EPS,
                                  ALU.mult, ALU.add).then_inc(s_a_var, 1)
                ch_a.end()

            def stage_a_apply(at):
                b, par, half = at
                dve.wait_ge(s_a_rstd, b + 1)
                if not first(b, 1):
                    dve.wait_ge(s_tx, KD * b)
                for c in range(CT):
                    dve.tensor_scalar(xhat[:, c, :], x_in[par][:, c, :], mv[:, 0, c, 0:1], rstd[:, 0, c:c + 1],
                                      ALU.subtract, ALU.mult).then_inc(s_xhat, 1)

            def general_scan(par):
                dve.memset(ssm_t[:], 0.0)
                dve.drain()
                with dve.Fori(0, L) as t:
                    dve.tensor_tensor(ssm_t[:], ssm_t[:], dec[:], ALU.mult)
                    dve.tensor_tensor(ssm_u[:], bmat[:], xs[par][:, :, bass.ds(t, 1)].to_broadcast([P, NC, NS]),
                                      ALU.mult)
                    dve.drain()
                    dve.scalar_tensor_tensor(out=ssm_t[:], in0=ssm_u[:], scalar=0.1, in1=ssm_t[:],
                                             op0=ALU.mult, op1=ALU.add)
                    dve.drain()
                    dve.tensor_scalar(ssm_t[:], ssm_t[:], CLIP, -CLIP, ALU.min, ALU.max)
                    dve.drain()
                    dve.tensor_tensor(ssm_u[:], ssm_t[:], cmat[:], ALU.mult)
                    dve.drain()
                    dve.tensor_reduce(state[:, :, bass.ds(t, 1)], ssm_u[:], AX_X, ALU.add)
                    dve.drain()
                for c in range(NC):
                    dve.tensor_scalar(state[:, c, :], state[:, c, :], CLIP, None, ALU.min)
                dve.drain()

            def scan_chunk(at, c):
                b, par, half = at
                wait_apart(dve, held, (s_flag, 1), (s_projc, 2 * NC * b + c + 1),
                           *([] if first(b, 1) else [(s_z, NC * (b - 1) + c + 1)]))
                with dve.If(is_general != 0):
                    if c == 0:
                        for n in range(NC):
                            dve.wait_ge(s_flag, 1)
                            dve.wait_ge(s_projc, 2 * NC * b + n + 1)
                            dve.tensor_scalar(xs[par][:, n, :], xs[par][:, n, :], CLIP, -CLIP, ALU.min, ALU.max)
                        dve.drain()
                        general_scan(par)
                with dve.Else():
                    dve.tensor_scalar(xs[par][:, c, :], xs[par][:, c, :], CLIP, -CLIP, ALU.min, ALU.max)
                    dve.drain()
                    dve.tensor_tensor_scan(state[:, c, :], decay_row[:, c, :], xs[par][:, c, :], 0.0,
                                           ALU.mult, ALU.add)
                    dve.drain()
                    dve.tensor_scalar(state[:, c, :], state[:, c, :], wsum[:, c:c + 1], CLIP, ALU.mult, ALU.min)
                dve.wait_ge(s_projc, 2 * NC * b + NC + c + 1)
                ch_b.link(dve.tensor_scalar(gate[par][:, c, :], gate[par][:, c, :], TANH_CLIP, -TANH_CLIP,
                                            ALU.min, ALU.max))
                ch_b.wait()
                dve.scalar_tensor_tensor(out=gate[par][:, c, :], in0=state[:, c, :], scalar=-CLIP,
                                         in1=gate[par][:, c, :], op0=ALU.max, op1=ALU.mult).then_inc(s_z, 1)

            def out_clip(at):
                b, par, half = at
                ch_c.begin(b)
                if not first(b, 1):
                    dve.wait_ge(s_xnew, CT * b)
                for h in range(2):
                    dve.wait_ge(s_omm, CT * b + (h + 1) * CT // 2)
                    dve.tensor_scalar(o[:, 2 * h:2 * h + 2, :],
                                      PO[h][:, :].rearrange("p (c d) -> p c d", d=D), CLIP, -CLIP,
                                      ALU.min, ALU.max).then_inc(s_o, 1)
                dve.wait_ge(s_o, 2 * (b + 1))
                ch_c.wait()
                norm_stats(ch_c, 1, o)
                dve.tensor_scalar(var[:, 1, :], mv[:, 1, :, 1], LN_EPS, None, ALU.add).then_inc(s_c_var, 1)
                for c in range(CT):
                    ch_c.link(dve.scalar_tensor_tensor(out=o[:, c, :], in0=o[:, c, :],
                                                       scalar=mv[:, 1, c, 0:1], in1=gout[:],
                                                       op0=ALU.subtract, op1=ALU.mult))

            def residual(at):
                b, par, half = at
                dve.wait_ge(s_c_rstd, 2 * b + 1)
                dve.wait_ge(s_resb, CT * (b + 1))
                ch_c.wait()
                for c in range(CT):
                    dve.scalar_tensor_tensor(out=x_res[par][:, c, :], in0=o[:, c, :],
                                             scalar=rstd[:, 1, c:c + 1], in1=x_res[par][:, c, :],
                                             op0=ALU.mult, op1=ALU.add).then_inc(s_xnew, 1)
                dve.wait_ge(s_xnew, CT * (b + 1))
                norm_stats(ch_c, 2, x_res[par])
                dve.tensor_scalar(var[:, 2, :], mv[:, 2, :, 1], LN_EPS, None, ALU.add).then_inc(s_c_var, 1)

            def expert_input(at):
                b, par, half = at
                dve.wait_ge(s_c_rstd, 2 * b + 2)
                if not first(b, 1):
                    dve.wait_ge(s_out[1 - par], 32 * (half + par))
                    dve.wait_ge(s_tr, KD * b)
                for c in range(CT):
                    dve.tensor_scalar(r[:, c, :], x_res[par][:, c, :], mv[:, 2, c, 0:1],
                                      rstd[:, 2, c:c + 1], ALU.subtract, ALU.mult).then_inc(s_r, 1)
                ch_c.end()

            def logits_less_max(at):
                b, par, half = at
                ch = ch_d
                ch.begin(b)
                ch.wait()
                dve.wait_ge(s_logit, b + 1)
                ch.link(dve.tensor_reduce(mx[:], m_logit, AX_X, ALU.max))
                ch.wait()
                dve.tensor_tensor(lg[:], m_logit, mx[:].unsqueeze(2).to_broadcast([P, CT, E]),
                                  ALU.subtract).then_inc(s_lg, 1)

            def choose(at):
                b, par, half = at
                ch = ch_d
                if not first(b, 1):
                    dve.wait_ge(s_s_dve, 4 * b)
                dve.wait_ge(s_ex, b + 1)
                ch.link(dve.tensor_reduce(den[:], ex[:], AX_X, ALU.add))
                ch.wait()
                ch.link(dve.reciprocal(mx[:], den[:]))
                ch.wait()
                ch.link(dve.tensor_tensor(prob[:], ex[:], mx[:].unsqueeze(2).to_broadcast([P, CT, E]), ALU.mult))
                ch.wait_apart(held, (s_const, 160))
                for c in range(CT):
                    ch.link(dve.max(top[:, c, :], prob[:, c, :]))
                ch.wait_apart(held, (s_const, 160))
                for c in range(CT):
                    ch.link(dve.max_index(top_i[:, c, :], top[:, c, :], prob[:, c, :]))
                ch.wait()
                ch.link(dve.tensor_copy(top_f[:], top_i[:, :, 0:TOP]))
                ch.wait()
                for k in range(TOP):
                    ins = dve.tensor_tensor(hot[:, k, :, :], iota8[:].unsqueeze(1).to_broadcast([P, CT, E]),
                                            top_f[:, :, k:k + 1].to_broadcast([P, CT, E]), ALU.is_equal)
                ch.link(ins)
                ch.wait()
                ch.link(dve.tensor_tensor(mask[:], hot[:, 0, :, :], hot[:, 1, :, :], ALU.add))
                for c in range(CT):
                    ch.wait()
                    ins = dve.tensor_tensor(before[:, c + 1, :], before[:, c, :], mask[:, c, :], ALU.add)
                    if c < CT - 1:
                        ch.link(ins)
                ins.then_inc(s_mask, 1)
                ch.end()

            def place(at):
                b, par, half = at
                ch = ch_s
                ch.begin(b)
                ch.wait()
                dve.wait_ge(s_rank, b + 1)
                if not first(b, 1):
                    dve.wait_ge(s_rankread, b)
                ch.link(dve.tensor_tensor(slot_f[:], m_rank[:, 0:CT, :],
                                          cnt[:].unsqueeze(1).to_broadcast([P, CT, E]), ALU.add))
                ch.wait()
                dve.tensor_tensor(cnt[:], cnt[:], m_rank[:, CT, :], ALU.add).then_inc(s_rankread, 1)
                for k in range(TOP):
                    ins = dve.tensor_tensor(pick[:, k, :, :], hot[:, k, :, :], slot_f[:], ALU.mult)
                ch.link(ins)
                ch.wait()
                ch.link(dve.tensor_reduce(slot_sum[:], pick[:], AX_X, ALU.add))
                if not first(b, 2):
                    dve.wait_ge(s_rows[par], 16 * TOP * CT * half)
                ch.wait()
                dve.tensor_copy(slot[par][:], slot_sum[:])
                for k in range(TOP):
                    dve.tensor_copy(row[par][:, k, :, 0], ids[:])
                    ins = dve.tensor_copy(row[par][:, k, :, 1].bitcast(F32), top[:, :, k])
                ins.then_inc(s_slot, 1)
                ch.link(dve.tensor_scalar(ids[:], ids[:], float(L), None, ALU.add))
                ch.end()

            def step(m, u):
                a, b, c, d, p = (lagged(m, u, n, NB) for n in range(5))
                if p:
                    place(p)
                if a:
                    stage_a(a)
                if b:
                    ch_b.begin(b[0])
                    scan_chunk(b, 0)
                if a:
                    stage_a_apply(a)
                if c:
                    out_clip(c)
                if d:
                    logits_less_max(d)
                if b:
                    scan_chunk(b, 1)
                if c:
                    residual(c)
                if d:
                    choose(d)
                if b:
                    scan_chunk(b, 2)
                if c:
                    expert_input(c)

            batches(dve, step)

            dve.wait_ge(s_rankread, NB)
            regions = iota8[0:1, :]
            t = s_tile_tab
            n = 0

            def chained(ins):
                nonlocal n
                ins.then_inc(t, 1)
                n += 1
                dve.wait_ge(t, n)

            chained(dve.tensor_scalar(n_e[:], regions, -float(REGION), None, ALU.mult))
            chained(dve.tensor_tensor(n_e[:], n_e[:], cnt[0:1, :], ALU.add))
            chained(dve.tensor_tensor(cmp_t, n_e[:].unsqueeze(2).to_broadcast([1, E, T // P]),
                                      step128[:].unsqueeze(1).to_broadcast([1, E, T // P]), ALU.is_gt))
            chained(dve.tensor_reduce(tiles_e[:], cmp_t, AX_X, ALU.add))
            chained(dve.tensor_tensor_scan(incl[:], ones8[:], tiles_e[:], 0.0, ALU.mult, ALU.add))
            chained(dve.tensor_tensor(past, tile_no[:].unsqueeze(2).to_broadcast([1, NT, E - 1]),
                                      incl[:, 0:E - 1].unsqueeze(1).to_broadcast([1, NT, E - 1]), ALU.is_ge))
            chained(dve.tensor_tensor(past_t, past,
                                      tiles_e[:, 0:E - 1].unsqueeze(1).to_broadcast([1, NT, E - 1]), ALU.mult))
            chained(dve.tensor_reduce(e_of[:], past, AX_X, ALU.add))
            chained(dve.tensor_reduce(start_of[:], past_t, AX_X, ALU.add))
            chained(dve.tensor_tensor(row_f[:], tile_no[:], start_of[:], ALU.subtract))
            chained(dve.tensor_scalar(row_f[:], row_f[:], float(P), None, ALU.mult))
            chained(dve.scalar_tensor_tensor(out=row_f[:], in0=e_of[:], scalar=float(REGION), in1=row_f[:],
                                             op0=ALU.mult, op1=ALU.add))
            dve.tensor_copy(tile_row[:], row_f[:]).then_inc(s_tiles, 1)
            dve.tensor_copy(tile_e[:], e_of[:]).then_inc(s_tiles, 1)

            def tile_step(m, u):
                if at := tile(m, u, 0):
                    j, par, _, _, _ = at
                    dve.wait_ge(s_silu, j + 1)
                    if not first(j, 2):
                        dve.wait_ge(s_yt, j - 1)
                    dve.tensor_tensor(act_y[par], [PT, PG][par][1][:, :], act_s[par], ALU.mult).then_inc(s_y, 1)

            tiles(dve, tile_step)

        @block.tensor
        def _(pe):
            pe.wait_ge(s_const, 160)
            pe.wait_ge(s_pool0, 16)
            for j in range(2 * NC):
                for k in range(KD):
                    ins = pe.matmul(m_bias[:, j:j + 1], wi[:, k, j * P:(j + 1) * P], bin_[:, k:k + 1],
                                    start=(k == 0), stop=(k == KD - 1))
            ins.then_inc(s_bias_mm, 1)
            pe.wait_ge(s_setup, 15)
            pe.wait_ge(s_biascopy, 1)
            pe.matmul(m_viol, viol[:], ones1[:], start=True, stop=True).then_inc(s_ready, 1)

            def step(m, u):
                if at := lagged(m, u, 2, NB):
                    b, par, half = at
                    pe.wait_ge(s_z, NC * (b + 1))
                    if not first(b, 1):
                        pe.wait_ge(s_o, 2 * b)
                    for c in range(CT):
                        for k in range(NC):
                            ins = pe.matmul(PO[c // 2][:, (c % 2) * D:(c % 2 + 1) * D],
                                            gate[par][:, k, c * P:(c + 1) * P], wo[:, k, :],
                                            start=(k == 0), stop=(k == NC - 1))
                        ins.then_inc(s_omm, 1)
                if at := lagged(m, u, 3, NB):
                    b, par, half = at
                    pe.wait_ge(s_r, CT * (b + 1))
                    for k in range(KD):
                        if not first(b, 1) or k > 0:
                            pe.wait_ge(s_trc, KD * b + k)
                        for c in range(CT):
                            ins = pe.transpose(PR[:, c * P:(c + 1) * P], r[:, c, k * P:(k + 1) * P], ident[:])
                        ins.then_inc(s_tr, 1)
                    pe.wait_ge(s_trc, KD * (b + 1))
                    if not first(b, 1):
                        pe.wait_ge(s_rankread, b)
                    for c in range(CT):
                        for k in range(KD):
                            ins = pe.matmul(m_logit[:, c, :], r_t[:, k, c * P:(c + 1) * P], rw[:, k, :],
                                            start=(k == 0), stop=(k == KD - 1))
                    ins.then_inc(s_logit, 1)
                if at := lagged(m, u, 0, NB):
                    b, par, half = at
                    for k in range(KD):
                        if k == 0:
                            pe.wait_ge(s_xhat, CT * (b + 1))
                        if not first(b, 1):
                            pe.wait_ge(s_txc, KD * (b - 1) + k + 1)
                        for c in range(CT):
                            ins = pe.transpose(PT[k][:, c * P:(c + 1) * P], xhat[:, c, k * P:(k + 1) * P], ident[:])
                        ins.then_inc(s_tx, 1)
                    pe.wait_ge(s_txc, KD * (b + 1))
                    for j in range(2 * NC):
                        if not (first(b, 1) and j < 2):
                            pe.wait_ge(s_projc, 2 * NC * b + j - 1)
                        for k in range(KD):
                            ins = pe.matmul(PG[j % 2][:, :], wi[:, k, j * P:(j + 1) * P], xhat_t[:, k, :],
                                            start=(k == 0), stop=(k == KD - 1))
                        ins.then_inc(s_proj, 1)
                if at := lagged(m, u, 3, NB):
                    b, par, half = at
                    pe.wait_ge(s_mask, b + 1)
                    pe.matmul(PM[:, 64:64 + (CT + 1) * E], onesb[:], before[:].rearrange("p c e -> p (c e)"),
                              start=True, stop=False)
                    pe.matmul(PM[:, 64:64 + CT * E], upper[:], mask[:].rearrange("p c e -> p (c e)"),
                              start=False, stop=True).then_inc(s_rank, 1)

            batches(pe, step)
            pe.wait_ge(s_wload, 16 * 2 * E)
            pe.wait_ge(s_tiles, 2)
            pe.wait_ge(s_rankread, NB)
            pe.wait_ge(s_projc, 2 * NC * NB)

            def gathered(at):
                j, par, uses, _, _ = at
                pe.wait_ge(s_xg[par], 16 * (uses + 1))
                if not first(j, 1):
                    pe.wait_ge(s_gtc, j)
                for k in range(KD):
                    ins = pe.transpose(PR[:, k * P:(k + 1) * P], xg[par][:, k * P:(k + 1) * P], ident[:])
                ins.then_inc(s_gt, 1)

            def hidden(at):
                j, par, _, _, _ = at
                e = pe.value_load(tile_e[0:1, bass.ds(j, 1)], min_val=0, max_val=E - 1)
                pe.wait_ge(s_gtc, j + 1)
                if not first(j, 2):
                    pe.wait_ge(s_y, j - 1)
                for h in range(2):
                    for k in range(KD):
                        ins = pe.matmul([PT, PG][par][h][:, :], xg_t[par][:, k, :],
                                        w1[:, k, bass.ds(e * I2 + h * I, I)],
                                        start=(k == 0), stop=(k == KD - 1))
                ins.then_inc(s_h, 1)

            def turned(at):
                j, par, _, _, _ = at
                pe.wait_ge(s_y, j + 1)
                if not first(j, 1):
                    pe.wait_ge(s_ytc, j)
                for k in range(KI):
                    ins = pe.transpose(PO[1][:, k * P:(k + 1) * P], act_y[par][:, k * P:(k + 1) * P], ident[:])
                ins.then_inc(s_yt, 1)

            def combined(at):
                j, par, _, _, _ = at
                e = pe.value_load(tile_e[0:1, bass.ds(j, 1)], min_val=0, max_val=E - 1)
                pe.wait_ge(s_ytc, j + 1)
                if not first(j, 1):
                    pe.wait_ge(s_yout, j)
                for k in range(KI):
                    ins = pe.matmul(PO[0][:, 0:D], y_t[par][:, k, :], w2[:, k, bass.ds(e * D, D)],
                                    start=(k == 0), stop=(k == KI - 1))
                ins.then_inc(s_mo, 1)

            def tile_step(m, u):
                now, last, nxt = (tile(m, u, n) for n in (0, 1, -1))
                if last:
                    turned(last)
                if now:
                    hidden(now)
                if nxt:
                    gathered(nxt)
                if last:
                    combined(last)

            gathered(tile(0, 0, 0))
            tiles(pe, tile_step, ahead=1)


def kernel(L0_attn_x, L0_attn_W_in, L0_attn_W_out, L0_attn_A_log, L0_attn_B, L0_attn_C, L0_attn_ln_in_g,
           L0_attn_ln_in_b, L0_attn_ln_out_g, L0_attn_ln_out_b, L0_ffn_w1, L0_ffn_w2, L0_ffn_router_w):
    import numpy as np
    import concourse.bacc as bacc
    from concourse.bass_utils import run_bass_kernel_spmd

    given = {
        "x": L0_attn_x,
        "w_in_t": np.transpose(L0_attn_W_in),
        "w_out_t": np.transpose(L0_attn_W_out),
        "a_log": L0_attn_A_log,
        "b_in": L0_attn_B,
        "c_out": L0_attn_C,
        "g_in": np.transpose(L0_attn_ln_in_g.reshape(-1, P)),
        "bias_in": np.transpose(L0_attn_ln_in_b.reshape(-1, P)),
        "g_out": L0_attn_ln_out_g,
        "bias_out": L0_attn_ln_out_b,
        "w1_t": np.transpose(L0_ffn_w1, (0, 2, 1)),
        "w2_t": np.transpose(L0_ffn_w2, (0, 2, 1)),
        "router_t": np.transpose(L0_ffn_router_w),
    }
    nc = bacc.Bacc("TRN2", target_bir_lowering=False, num_devices=1)
    arrays, args = {}, {}
    for name, a in given.items():
        arrays[name] = np.ascontiguousarray(a)
        args[name] = nc.dram_tensor(name, a.shape, mybir.dt.from_np(arrays[name].dtype), kind="ExternalInput").ap()
    out = nc.dram_tensor("out", L0_attn_x.shape, F32, kind="ExternalOutput").ap()
    build(nc, **args, out=out)
    got = run_bass_kernel_spmd(nc, [arrays], core_ids=[0])
    return got.results[0]["out"]
```

```python
from contextlib import ExitStack

import concourse.bass as bass
from concourse import mybir

F32 = mybir.dt.float32
BF16 = mybir.dt.bfloat16
F16 = mybir.dt.float16
I32 = mybir.dt.int32
U32 = mybir.dt.uint32
ALU = mybir.AluOpType
ACT = mybir.ActivationFunctionType
AX_X = mybir.AxisListType.X

P = 128
LN_EPS = 1e-5
CLIP = 5.0
TANH_CLIP = 0.9999092042625951
PAD_TOKEN = 1 << 20
X_SCALE_LOG = 11
X_SCALE = float(1 << X_SCALE_LOG)


def lagged(m, u, d, count, n=2):
    if isinstance(m, int) and not 0 <= n * m + u - d < count:
        return None
    return n * m + (u - d), (u - d) % n, m + (u - d) // n


def first(b, n):
    return isinstance(b, int) and b < n


def wait_apart(eng, held, met, *waits):
    ready = []
    for n, (sem, value) in enumerate(waits):
        if not isinstance(value, int):
            at = held.get((eng.engine, n)) or held.setdefault((eng.engine, n), eng.alloc_register(f"apart{n}"))
            eng.reg_mov(at, value)
            value = at
        ready.append((sem, value))
    eng.wait_ge(*met)
    for sem, value in ready:
        eng.wait_ge(sem, value)


class Chain:

    def __init__(self, eng, sem, per):
        self.eng, self.sem, self.per = eng, sem, per

    def begin(self, b):
        self.b, self.k = b, 0

    def link(self, ins):
        ins.then_inc(self.sem, 1)
        self.k += 1
        assert self.k <= self.per

    def wait(self):
        if not first(self.b, 1) or self.k:
            self.eng.wait_ge(self.sem, self.per * self.b + self.k)

    def step(self, ins):
        self.link(ins)
        self.wait()

    def wait_apart(self, held, met):
        wait_apart(self.eng, held, met, (self.sem, self.per * self.b + self.k))

    def end(self):
        assert self.k == self.per, (self.k, self.per)


def build(nc, x, w_in_t, w_out_t, a_log, b_in, c_out, g_in, bias_in, g_out, bias_out,
          w1_t, w2_t, router_t, out):
    NB, L, D = x.shape
    CT = L // P
    KD = D // P
    DI = w_in_t.shape[1] // 2
    NC = DI // P
    NS = a_log.shape[1]
    E, _, I2 = w1_t.shape
    I = I2 // 2
    KI = I // P
    T = NB * L
    TOP = 2
    NT = T * TOP // P + E - 1
    REGION = T
    ROWS = E * REGION + P * E
    U = 8

    x_v = x.rearrange("b (c p) d -> b p c d", p=P)
    out_v = out.rearrange("b (c p) d -> b p c d", p=P)
    out_rows = out.rearrange("b l d -> (b l) d")
    r_rows = nc.dram_tensor("expert_input_rows", [T, D], F32).ap()
    r_v = r_rows.rearrange("(b c p) d -> b p c d", p=P, c=CT)
    table = nc.dram_tensor("slot_table", [ROWS, 2], I32).ap()

    w1_rows = w1_t.rearrange("e (k p) n -> e p k n", p=P)
    w2_rows = w2_t.rearrange("e (k p) n -> e p k n", p=P)

    with ExitStack() as ctx:
        def sb(name, shape, dt=F32):
            return ctx.enter_context(nc.sbuf_tensor(name, shape, dt))

        def psum(name):
            return ctx.enter_context(nc.psum_tensor(name, [P, 512], F32))

        def sem(name):
            return ctx.enter_context(nc.semaphore(name))

        w1h = sb("w1h", [P, KD, E * I2], F16)
        w1l = sb("w1l", [P, KD, E * I2], F16)
        w2h = sb("w2h", [P, KI, E * D], F16)
        w2l = sb("w2l", [P, KI, E * D], F16)
        stage = sb("stage", [P, KD, I2])
        stage2 = sb("stage2", [P, KI, D])
        wi = stage[:].rearrange("p k n -> p (k n)")[:, 0:KD * 2 * DI].rearrange("p (k n) -> p k n", k=KD)
        wih = sb("wih", [P, KD, 2 * DI], F16)
        wil = sb("wil", [P, KD, 2 * DI], F16)
        squares = sb("squares", [P, 2])
        square_sum = sb("square_sum", [P, 1])
        half_exp = sb("half_exp", [P, 1], I32)
        w_scale = sb("w_scale", [P, 2], I32)
        wi_inv = sb("wi_inv", [P, 1], I32)
        w1_inv = sb("w1_inv", [P, E], I32)
        w2_inv = sb("w2_inv", [P, 1], I32)
        row_max = sb("row_max", [P, 2])
        row_exp = sb("row_exp", [P, 1], I32)
        y_exp = sb("y_exp", [P, E], I32)
        up_scale = sb("up_scale", [P, E], I32)
        y_inv = sb("y_inv", [P, E], I32)
        wo = sb("wo", [P, NC, D])
        rw = sb("rw", [P, KD, E])
        gout = sb("gout", [P, D])
        bout = sb("bout", [P, D])
        gin = sb("gin", [P, KD])
        bin_ = sb("bin", [P, KD])
        ident = sb("ident", [P, P])
        upper = sb("upper", [P, P], BF16)
        onesb = sb("onesb", [P, P], BF16)
        onesf = sb("onesf", [P, P])
        minus_id = sb("minus_id", [P, P], F16)
        minus1 = sb("minus1", [P, CT])
        mhalf = sb("mhalf", [P, CT])
        iota8 = sb("iota8", [P, E])
        ids = sb("ids", [P, CT])
        alog = sb("alog", [P, NC, NS])
        bmat = sb("bmat", [P, NC, NS])
        cmat = sb("cmat", [P, NC, NS])
        dec = sb("dec", [P, NC, NS])
        ssm_t = sb("ssm_t", [P, NC, NS])
        ssm_u = sb("ssm_u", [P, NC, NS])
        wsum = sb("wsum", [P, NC])
        viol = sb("viol", [P, 1])
        w_eff = sb("w_eff", [P, NC])
        flag = sb("flag", [P, 1])
        general = sb("general", [1, 1], I32)
        pbias = sb("pbias", [P, 2 * NC])
        decay_row = sb("decay_row", [P, NC, L])
        x_in = [sb(f"x_in{i}", [P, CT, D]) for i in range(2)]
        x_res = [sb(f"x_res{i}", [P, CT, D]) for i in range(2)]
        xhat = sb("xhat", [P, CT, D])
        xh_t = sb("xh_t", [P, KD, L], F16)
        xl_t = sb("xl_t", [P, KD, L], F16)
        xs = [sb(f"xs{i}", [P, NC, L]) for i in range(2)]
        gate = [sb(f"gate{i}", [P, NC, L]) for i in range(2)]
        state = sb("state", [P, NC, L])
        o = sb("o", [P, CT, D])
        r = sb("r", [P, CT, D])
        r_t = sb("r_t", [P, KD, L + 8])
        stats = sb("stats", [P, 3, CT, 6])
        mv = sb("mv", [P, 3, CT, 2])
        var = sb("var", [P, 3, CT])
        rstd = sb("rstd", [P, 3, CT])
        mr = sb("mr", [P, 3, CT])
        nmr = sb("nmr", [P, 3, CT])
        lg = sb("lg", [P, CT, E])
        mx = sb("mx", [P, CT])
        ex = sb("ex", [P, CT, E])
        den = sb("den", [P, CT])
        prob = sb("prob", [P, CT, E])
        top = sb("top", [P, CT, 8])
        top_i = sb("top_i", [P, CT, 8], U32)
        top_f = sb("top_f", [P, CT, TOP])
        hot = sb("hot", [P, TOP, CT, E])
        mask = sb("mask", [P, CT + 1, E], BF16)
        slot_f = sb("slot_f", [P, CT, E])
        pick = sb("pick", [P, TOP, CT, E])
        slot_sum = sb("slot_sum", [P, TOP, CT])
        slot = [sb(f"slot{i}", [P, TOP, CT], U32) for i in range(2)]
        row = [sb(f"row{i}", [P, TOP, CT, 2], I32) for i in range(2)]
        cnt = sb("cnt", [P, E])
        n_e = sb("n_e", [1, E])
        step128 = sb("step128", [1, T // P])
        cmp_t = x_in[0][0:1, 0:2, :].rearrange("p c d -> p (c d)").rearrange("p (e n) -> p e n", e=E)
        tiles_e = sb("tiles_e", [1, E])
        ones8 = sb("ones8", [1, E])
        incl = sb("incl", [1, E])
        tile_no = sb("tile_no", [1, NT])
        past, past_t = (x_in[i][0:1, :, :].rearrange("p c d -> p (c d)")[:, 0:NT * (E - 1)]
                        .rearrange("p (n e) -> p n e", e=E - 1) for i in range(2))
        e_of = sb("e_of", [1, NT])
        start_of = sb("start_of", [1, NT])
        row_f = sb("row_f", [1, NT])
        tile_e = sb("tile_e", [1, NT], I32)
        tile_row = sb("tile_row", [1, NT], I32)
        tb = [sb(f"tb{i}", [P, 2], I32) for i in range(U)]
        xgh = [xh_t[:, i, 0:D].rearrange("p (k q) -> p k q", k=KD) for i in range(2)]
        xgl = [xl_t[:, i, 0:D].rearrange("p (k q) -> p k q", k=KD) for i in range(2)]
        act_s = [xs[i][:, 1, 0:I] for i in range(2)]
        act_y = [xs[i][:, 2, 0:I] for i in range(2)]
        yth, ytl = ([gate[i][:, n, 0:I // 2].bitcast(F16).rearrange("p (k q) -> p k q", k=KI)
                     for i in range(2)] for n in range(2))
        xg = [state[:, i, 0:D] for i in range(2)]
        y_out = [state[:, i, D:2 * D] for i in range(2)]
        pad_src = r_t[:, :, :].rearrange("p k n -> p (k n)")[:, 0:ROWS // P * 2].bitcast(I32)

        PT = [psum("PT0"), psum("PT1")]
        PG = [psum("PG0"), psum("PG1")]
        PO = [psum("PO0"), psum("PO1")]
        PR = psum("PR")
        PM = psum("PM")
        m_logit = PM[:, 0:CT * E].rearrange("p (c e) -> p c e", e=E)
        m_rank = PM[:, 64:64 + (CT + 1) * E].rearrange("p (c e) -> p c e", e=E)
        m_bias = PM[:, 128:128 + 2 * NC]
        m_viol = PM[:, 140:141]
        m_square = PT[0][:, 0:1]

        s_const = sem("s_const")
        s_x = [sem(f"s_x{i}") for i in range(2)]
        s_xr = [sem(f"s_xr{i}") for i in range(2)]
        s_out = [sem(f"s_out{i}") for i in range(2)]
        s_padset = sem("s_padset")
        s_pad = sem("s_pad")
        s_pool0 = sem("s_pool0")
        s_setup = sem("s_setup")
        s_exp0 = sem("s_exp0")
        s_wi_sq = sem("s_wi_sq")
        s_wi_sum = sem("s_wi_sum")
        s_wi_scale = sem("s_wi_scale")
        s_wi_h = sem("s_wi_h")
        s_wi_l = sem("s_wi_l")
        s_stage = sem("s_stage")
        s_stage2 = sem("s_stage2")
        s_w2_sq = sem("s_w2_sq")
        s_w2_sum = sem("s_w2_sum")
        s_w2_scale = sem("s_w2_scale")
        s_w2_chain = sem("s_w2_chain")
        s_w2_h = sem("s_w2_h")
        s_w2_l = sem("s_w2_l")
        s_row_sq = sem("s_row_sq")
        s_row_max = sem("s_row_max")
        s_row_chain = sem("s_row_chain")
        s_y_inv = sem("s_y_inv")
        s_y_l = sem("s_y_l")
        s_w1_sq = sem("s_w1_sq")
        s_w1_sum = sem("s_w1_sum")
        s_w1_scale = sem("s_w1_scale")
        s_w1_chain = sem("s_w1_chain")
        s_w1_h = sem("s_w1_h")
        s_w1_l = sem("s_w1_l")
        s_norm = sem("s_norm")
        s_gain = sem("s_gain")
        s_pool_a = sem("s_pool_a")
        s_pool_c = sem("s_pool_c")
        s_pool_r = sem("s_pool_r")
        s_r_var = sem("s_r_var")
        s_r_rstd = sem("s_r_rstd")
        s_r_dve = sem("s_r_dve")
        s_low = sem("s_low")
        s_xg_l = sem("s_xg_l")
        s_bias_mm = sem("s_bias_mm")
        s_ready = sem("s_ready")
        s_biascopy = sem("s_biascopy")
        s_flag = sem("s_flag")
        s_a_dve = sem("s_a_dve")
        s_a_var = sem("s_a_var")
        s_a_rstd = sem("s_a_rstd")
        s_xhat = sem("s_xhat")
        s_tx = sem("s_tx")
        s_txc = sem("s_txc")
        s_proj = sem("s_proj")
        s_projc = sem("s_projc")
        s_b_dve = sem("s_b_dve")
        s_z = sem("s_z")
        s_omm = sem("s_omm")
        s_o = sem("s_o")
        s_c_dve = sem("s_c_dve")
        s_c_var = sem("s_c_var")
        s_c_rstd = sem("s_c_rstd")
        s_resb = sem("s_resb")
        s_xnew = sem("s_xnew")
        s_r = sem("s_r")
        s_d_dve = sem("s_d_dve")
        s_s_dve = sem("s_s_dve")
        s_tr = sem("s_tr")
        s_trc = sem("s_trc")
        s_logit = sem("s_logit")
        s_lg = sem("s_lg")
        s_ex = sem("s_ex")
        s_mask = sem("s_mask")
        s_rank = sem("s_rank")
        s_rankread = sem("s_rankread")
        s_slot = sem("s_slot")
        s_rows = [sem(f"s_rows{i}") for i in range(2)]
        s_tiles = sem("s_tiles")
        s_tile_tab = sem("s_tile_tab")
        s_tb = [sem(f"s_tb{i}") for i in range(U)]
        s_xgset = sem("s_xgset")
        s_xg = [sem(f"s_xg{i}") for i in range(2)]
        s_gt = sem("s_gt")
        s_gtc = sem("s_gtc")
        s_hg = sem("s_hg")
        s_h = sem("s_h")
        s_silu = sem("s_silu")
        s_y = sem("s_y")
        s_yt = sem("s_yt")
        s_ytc = sem("s_ytc")
        s_mo = sem("s_mo")
        s_yout = sem("s_yout")
        s_add = [sem(f"s_add{i}") for i in range(2)]

        held = {}
        SETUP = 20
        block = ctx.enter_context(nc.Block())

        STATS, PROJECT, SCAN, UNPROJECT, RESIDUAL, ROUTE, PLACE = range(7)
        LAGS = PLACE
        W2 = 2
        PEEL = 8

        def w1_part(part, e):
            return part[:, :, bass.ds(e * I2, I2)]

        def w2_part(part, e):
            return part[:, :, bass.ds(e * D, D)]

        def batches(eng, step):
            for s in range(PEEL):
                step(s // 2, s % 2)
            with eng.Fori(PEEL // 2, NB // 2) as m:
                for u in range(2):
                    step(m, u)
            for s in range(NB, NB + LAGS):
                step(s // 2, s % 2)

        def tiles(eng, step, ahead=0):
            last = NT // U - (1 if ahead else 0)
            for s in range(U):
                step(0, s)
            with eng.Fori(1, last) as m:
                for u in range(U):
                    step(m, u)
            for s in range(U * last, NT + 2):
                step(s // U, s % U)

        def tile(m, u, d):
            at = lagged(m, u, d, NT, U)
            return at and (at[0], at[1] % 2, at[2] * (U // 2) + at[1] // 2, at[1], at[2])

        @block.sync
        def _(sp):
            def load_x(at):
                b, par, half = at
                if not first(b, 2):
                    sp.wait_ge(s_xhat, CT * (b - 1))
                sp.dma_start(x_in[par][:, :, :], x_v[b]).then_inc(s_x[par], 16)

            load_x((0, 0, 0))
            for dst, src in ((wi[:, :, :], w_in_t.rearrange("(k p) n -> p k n", p=P)),
                             (gin[:, :], g_in),
                             (bin_[:, :], bias_in),
                             (alog[:, :, :], a_log.rearrange("(c p) d -> p c d", p=P)),
                             (bmat[:, :, :], b_in.rearrange("(c p) d -> p c d", p=P)),
                             (cmat[:, :, :], c_out.rearrange("(c p) d -> p c d", p=P)),
                             (wo[:, :, :], w_out_t.rearrange("(c p) n -> p c n", p=P)),
                             (rw[:, :, :], router_t.rearrange("(k p) e -> p k e", p=P)),
                             (gout[:, :], g_out.partition_broadcast(P)),
                             (bout[:, :], bias_out.partition_broadcast(P))):
                sp.dma_start(dst, src).then_inc(s_const, 16)
            load_x((1, 1, 0))
            sp.wait_ge(s_padset, 1)
            sp.dma_start(table.rearrange("(p n) t -> p (n t)", p=P), pad_src).then_inc(s_pad, 16)
            sp.wait_ge(s_pad, 16)

            def load_w1(e):
                if first(e, 1):
                    sp.wait_ge(s_wi_l, 1)
                else:
                    sp.wait_ge(s_w1_l, e)
                sp.dma_start(stage[:, :, :], w1_rows[e]).then_inc(s_stage, 16)

            def load_w2(e):
                if not first(e, 1):
                    sp.wait_ge(s_w2_l, e)
                sp.dma_start(stage2[:, :, :], w2_rows[e]).then_inc(s_stage2, 16)

            def step(m, u):
                if (at := lagged(m, u, -1, NB)) and not first(at[0], 2):
                    load_x(at)
                if lagged(m, u, 0, NB):
                    (load_w1, load_w2)[u](m)
                if at := lagged(m, u, UNPROJECT, NB):
                    b, par, half = at
                    if not first(b, 2):
                        sp.wait_ge(s_out[par], 32 * half)
                    sp.dma_start(x_res[par][:, :, :], x_v[b]).then_inc(s_xr[par], 16)
                if at := lagged(m, u, RESIDUAL, NB):
                    b, par, half = at
                    sp.wait_ge(s_xnew, b + 1)
                    sp.dma_start(out_v[b], x_res[par][:, :, :]).then_inc(s_out[par], 16)
                    sp.wait_ge(s_r, CT * (b + 1))
                    sp.dma_start(r_v[b], r[:, :, :]).then_inc(s_out[par], 16)

            for s in range(PEEL):
                step(s // 2, s % 2)
            with sp.Fori(PEEL // 2, NB // 2 - 1) as m:
                for u in range(2):
                    step(m, u)
            for s in range(NB - 2, NB + LAGS):
                step(s // 2, s % 2)

            sp.wait_ge(s_tiles, 2)
            for i in range(2):
                sp.wait_ge(s_rows[i], 16 * TOP * CT * NB // 2)

            def load_rows(m, i):
                j = U * m + i
                if not first(j, U):
                    sp.wait_ge(s_add[i % 2], 16 * (U // 2 * (m - 1) + i // 2 + 1))
                at = sp.value_load(tile_row[0:1, bass.ds(j, 1)], min_val=0, max_val=ROWS - P)
                sp.dma_start(tb[i][:, :], table[bass.ds(at, P), :]).then_inc(s_tb[i], 16)

            for i in range(U):
                load_rows(0, i)
            with sp.Fori(1, NT // U) as m:
                for i in range(U):
                    load_rows(m, i)
            for j in range(NT // U * U, NT):
                load_rows(j // U, j % U)
            for i in range(2):
                sp.wait_ge(s_add[i], 16 * ((NT + 1 - i) // 2))

        @block.gpsimd
        def _(pool):
            for t, v in ((ident, 0.0), (upper, 0.0), (onesb, 1.0), (onesf, 1.0), (minus_id, 0.0),
                         (minus1, -1.0), (mhalf, -0.5), (decay_row, 1.0), (ones8, 1.0)):
                pool.memset(t[:], v).then_inc(s_pool0, 1)
            pool.memset(pad_src, 0).then_inc(s_pool0, 1)
            pool.memset(mask[:], 0.0).then_inc(s_pool0, 1)
            pool.wait_ge(s_pool0, 11)
            pool.affine_select(out=ident[:], in_=ident[:], compare_op=ALU.not_equal, fill=1.0,
                               base=0, pattern=[[-1, P]], channel_multiplier=1).then_inc(s_pool0, 1)
            pool.affine_select(out=minus_id[:], in_=minus_id[:], compare_op=ALU.not_equal, fill=-1.0,
                               base=0, pattern=[[-1, P]], channel_multiplier=1).then_inc(s_pool0, 1)
            pool.affine_select(out=upper[:], in_=upper[:], compare_op=ALU.is_ge, fill=1.0,
                               base=0, pattern=[[-1, P]], channel_multiplier=1).then_inc(s_pool0, 1)
            pool.memset(pad_src.rearrange("p (n t) -> p n t", t=2)[:, :, 0], PAD_TOKEN).then_inc(s_padset, 1)
            pool.iota(iota8[:], pattern=[[1, E]], base=0, channel_multiplier=0,
                      allow_small_or_imprecise_dtypes=True).then_inc(s_pool0, 1)
            pool.iota(ids[:], pattern=[[P, CT]], base=0, channel_multiplier=1,
                      allow_small_or_imprecise_dtypes=True).then_inc(s_pool0, 1)
            pool.iota(cnt[:], pattern=[[REGION, E]], base=0, channel_multiplier=0,
                      allow_small_or_imprecise_dtypes=True).then_inc(s_pool0, 1)
            pool.iota(step128[:], pattern=[[P, T // P]], base=0, channel_multiplier=0,
                      allow_small_or_imprecise_dtypes=True).then_inc(s_pool0, 1)
            pool.iota(tile_no[:], pattern=[[1, NT]], base=0, channel_multiplier=0,
                      allow_small_or_imprecise_dtypes=True).then_inc(s_pool0, 1)
            pool.wait_ge(s_const, 160)

            def scatter(at, first_k, count):
                b, par, half = at
                for n in range(first_k, first_k + count):
                    k, c = divmod(n, CT)
                    pool.indirect_dma_start(
                        out=table, out_offset=bass.IndirectOffsetOnAxis(ap=slot[par][:, k, c:c + 1], axis=0),
                        in_=row[par][:, k, c, :], in_offset=None).then_inc(s_rows[par], 16)

            def roots(at, n, sem_var, sem_rstd, sem_own, sem_read):
                b = at[0]
                pool.wait_ge(sem_var, b + 1)
                if not first(b, 1):
                    pool.wait_ge(sem_read, CT * b)
                pool.tensor_tensor(rstd[:, n, :], var[:, n, :], mhalf[:], ALU.pow).then_inc(sem_own, 1)
                pool.wait_ge(sem_own, 2 * b + 1)
                pool.tensor_tensor(mr[:, n, :], mv[:, n, :, 0], rstd[:, n, :], ALU.mult).then_inc(sem_own, 1)
                pool.wait_ge(sem_own, 2 * b + 2)
                pool.tensor_tensor(nmr[:, n, :], mr[:, n, :], minus1[:], ALU.mult).then_inc(sem_rstd, 1)

            def step(m, u):
                at_a, at_w, at_r, at_s = (lagged(m, u, n, NB) for n in (STATS, UNPROJECT, RESIDUAL, PLACE))
                if at_r:
                    pool.wait_ge(s_norm, CT * (at_r[0] + 1))
                    pool.tensor_tensor(o[:], o[:], gout[:].unsqueeze(1).to_broadcast([P, CT, D]),
                                       ALU.mult).then_inc(s_gain, 1)
                if at_a:
                    roots(at_a, 0, s_a_var, s_a_rstd, s_pool_a, s_xhat)
                if at_s:
                    wait_apart(pool, held, (s_pad, 16), (s_slot, at_s[0] + 1))
                    scatter(at_s, 0, 3)
                if at_r:
                    roots(at_r, 2, s_r_var, s_r_rstd, s_pool_r, s_r)
                if at_s:
                    scatter(at_s, 3, 3)
                if at_w:
                    roots(at_w, 1, s_c_var, s_c_rstd, s_pool_c, s_norm)
                if at_s:
                    scatter(at_s, 6, 2)
                if at_w:
                    b, par, half = at_w
                    pool.wait_ge(s_xr[par], 16 * (half + 1))
                    pool.tensor_tensor(x_res[par][:, :, :], x_res[par][:, :, :],
                                       bout[:].unsqueeze(1).to_broadcast([P, CT, D]), ALU.add).then_inc(s_resb, 1)

            batches(pool, step)

            for i in range(2):
                pool.wait_ge(s_out[i], 32 * (NB // 2))
            for i in range(2):
                pool.memset(xg[i], 0.0).then_inc(s_xgset, 1)
            pool.wait_ge(s_xgset, 2)

            def gather(at):
                j, par, uses, i, tb_uses = at
                waits = [(s_tb[i], 16 * (tb_uses + 1))] + ([] if first(j, 2) else [(s_gt, j - 1)])
                wait_apart(pool, held, (s_pad, 16), *waits)
                pool.indirect_dma_start(
                    out=xg[par], out_offset=None, in_=r_rows,
                    in_offset=bass.IndirectOffsetOnAxis(ap=tb[i][:, 0:1].bitcast(U32), axis=0),
                    bounds_check=T - 1, oob_is_err=False).then_inc(s_xg[par], 16)

            def add(at):
                j, par, uses, i, tb_uses = at
                waits = [(s_yout, j + 1)] + ([] if first(j, 1) else [(s_add[1 - par], 16 * (uses + par))])
                wait_apart(pool, held, (s_pad, 16), *waits)
                pool.indirect_dma_start(
                    out=out_rows, out_offset=bass.IndirectOffsetOnAxis(ap=tb[i][:, 0:1].bitcast(U32), axis=0),
                    in_=y_out[par], in_offset=None,
                    bounds_check=T - 1, oob_is_err=False, compute_op=ALU.add).then_inc(s_add[par], 16)

            def tile_step(m, u):
                if at := tile(m, u, -2):
                    gather(at)
                if at := tile(m, u, 2):
                    add(at)

            for j in range(2):
                gather(tile(0, j, 0))
            tiles(pool, tile_step, ahead=2)

        @block.scalar
        def _(act):
            act.wait_ge(s_setup, 1)
            act.activation(ssm_u[:, :, :], ssm_t[:, :, :], ACT.Exp).then_inc(s_exp0, 1)
            act.wait_ge(s_bias_mm, 1)
            act.copy(pbias[:], m_bias).then_inc(s_biascopy, 1)
            act.wait_ge(s_biascopy, 1)
            act.wait_ge(s_setup, SETUP)
            act.activation(wih[:], wi, ACT.Square, accum_out=squares[:, 0:1]).then_inc(s_wi_sq, 1)
            act.wait_ge(s_wi_scale, 4)
            act.activation(wih[:], wi, ACT.Copy, scale=w_scale[:, 0:1].bitcast(F32)).then_inc(s_wi_h, 1)

            def normed(at, n, dst, src, sem_rstd, sem, tiles_c=range(CT)):
                b = at[0]
                if tiles_c[0] == 0:
                    act.wait_ge(sem_rstd, b + 1)
                for c in tiles_c:
                    act.activation(dst[:, c, :], src[:, c, :], ACT.Identity, scale=rstd[:, n, c:c + 1],
                                   bias=nmr[:, n, c:c + 1]).then_inc(sem, 1)

            def step(m, u):
                at_w1, at_w2, at_a, at_r, at_d = (lagged(m, u, n, NB)
                                                  for n in (STATS, W2, PROJECT, RESIDUAL, ROUTE))

                def turned_r(k):
                    act.wait_ge(s_tr, KD * at_d[0] + k + 1)
                    act.copy(r_t[:, k, 0:L], PR[:, :]).then_inc(s_trc, 1)

                def exponentials():
                    act.wait_ge(s_lg, at_d[0] + 1)
                    act.activation(ex[:, :, :], lg[:, :, :], ACT.Exp, scale=1.0 / X_SCALE).then_inc(s_ex, 1)

                def weight_high(n):
                    if at_w1 and u == 1:
                        if n == 0:
                            wait_apart(act, held, (s_const, 160), (s_w1_scale, m + 1))
                        k = slice(n * KD // 2, (n + 1) * KD // 2)
                        act.activation(w1_part(w1h, m)[:, k], stage[:, k], ACT.Copy,
                                       scale=w_scale[:, 0:1].bitcast(F32)).then_inc(s_w1_h, 1)
                    if at_w2 and u == 0:
                        if n == 0:
                            wait_apart(act, held, (s_const, 160), (s_w2_scale, m))
                        k = slice(n * KI // 2, (n + 1) * KI // 2)
                        act.activation(w2_part(w2h, m - 1)[:, k], stage2[:, k], ACT.Copy,
                                       scale=w_scale[:, 1:2].bitcast(F32)).then_inc(s_w2_h, 1)

                def r_tile(c):
                    b, par, half = at_r
                    if c == 0 and not first(b, 1):
                        act.wait_ge(s_out[1 - par], 32 * (half + par))
                        act.wait_ge(s_tr, KD * b)
                    normed(at_r, 2, r, x_res[par], s_r_rstd, s_r, range(c, c + 1))

                if at_a:
                    b, par, half = at_a
                    if not first(b, 1):
                        act.wait_ge(s_tx, KD * b)
                    normed(at_a, 0, xhat, x_in[par], s_a_rstd, s_xhat)
                    for k in range(KD):
                        act.wait_ge(s_tx, KD * b + k + 1)
                        act.copy(xh_t[:, k, :], PT[k][:, :]).then_inc(s_txc, 1)
                if at_r:
                    normed(at_r, 1, o, o, s_c_rstd, s_norm)
                if at_d:
                    turned_r(0)
                if at_a:
                    for k in range(KD):
                        act.wait_ge(s_low, KD * b + k + 1)
                        act.copy(xl_t[:, k, :], PT[k][:, :]).then_inc(s_txc, 1)
                if at_d:
                    turned_r(1)
                for j in range(2 * NC):
                    if at_d and j == 4:
                        exponentials()
                    if at_a:
                        act.wait_ge(s_proj, 2 * NC * b + j + 1)
                        dst = xs[par] if j < NC else gate[par]
                        act.activation(dst[:, j % NC, :], PG[j % 2][:, :], ACT.Identity if j < NC else ACT.Tanh,
                                       bias=pbias[:, j:j + 1], scale=wi_inv[:].bitcast(F32)).then_inc(s_projc, 1)
                    if j in (1, 2):
                        weight_high(j - 1)
                    if at_r and j >= 4:
                        r_tile(j - 4)
                if at_r:
                    r_tile(CT - 2)
                    r_tile(CT - 1)
                if at_w1 and u == 0:
                    act.wait_ge(s_stage, 16 * (m + 1))
                    act.activation(w1_part(w1l, m).bitcast(BF16), stage[:], ACT.Square,
                                   accum_out=squares[:, 0:1]).then_inc(s_w1_sq, 1)
                if at_w1 and u == 1:
                    act.wait_ge(s_stage2, 16 * (m + 1))
                    act.activation(w2_part(w2l, m), stage2[:], ACT.Square,
                                   accum_out=squares[:, 1:2]).then_inc(s_w2_sq, 1)

            batches(act, step)

            def copy_gathered(at):
                j, par, _, _, _ = at
                act.wait_ge(s_gt, j + 1)
                act.copy(xgh[par], PR[:, 0:D].rearrange("p (k q) -> p k q", k=KD)).then_inc(s_gtc, 1)

            def tile_step(m, u):
                now, last, nxt = (tile(m, u, n) for n in (0, 1, -1))
                if now:
                    e = act.value_load(tile_e[0:1, bass.ds(now[0], 1)], min_val=0, max_val=E - 1)
                if nxt:
                    copy_gathered(nxt)
                if last:
                    j, par, _, _, _ = last
                    act.wait_ge(s_yt, j + 1)
                    if not first(j, 2):
                        act.wait_ge(s_mo, j - 1)
                    act.copy(yth[par], PO[1][:, :].rearrange("p (k q) -> p k q", k=KI)).then_inc(s_ytc, 1)
                if now:
                    j, par, _, _, _ = now
                    wait_apart(act, held, (s_const, 160), (s_hg, j + 1))
                    act.activation(act_s[par], [PT, PG][par][0][:, :], ACT.Silu,
                                   scale=w1_inv[:, bass.ds(e, 1)].bitcast(F32)).then_inc(s_silu, 1)

            act.wait_ge(s_tiles, 2)
            copy_gathered(tile(0, 0, 0))
            tiles(act, tile_step, ahead=1)

        @block.vector
        def _(dve):
            setup = Chain(dve, s_setup, SETUP)
            setup.begin(0)
            dve.wait_ge(s_const, 160)
            setup.step(dve.tensor_scalar(ssm_t[:], alog[:], -5.0, 0.0, ALU.max, ALU.min))
            dve.wait_ge(s_exp0, 1)
            setup.step(dve.tensor_scalar(dec[:], ssm_u[:], -1.0, -2.0, ALU.mult, ALU.max))
            setup.step(dve.tensor_scalar(dec[:], dec[:], -0.01, 0.9, ALU.min, ALU.mult))
            setup.step(dve.tensor_tensor(ssm_t[:], bmat[:], cmat[:], ALU.mult))
            setup.step(dve.tensor_reduce(wsum[:], ssm_t[:], AX_X, ALU.add))
            setup.step(dve.tensor_scalar(wsum[:], wsum[:], 0.1, None, ALU.mult))
            dve.wait_ge(s_pool0, 19)
            for c in range(NC):
                ins = dve.tensor_scalar(decay_row[:, c, 1:L], decay_row[:, c, 1:L], dec[:, c, 0:1], None, ALU.mult)
            setup.step(ins)
            setup.step(dve.memset(decay_row[:, :, 0:1], 0.0))
            setup.step(dve.scalar_tensor_tensor(out=ssm_t[:], in0=bmat[:], scalar=-1.0, in1=bmat[:],
                                                op0=ALU.mult, op1=ALU.max))
            setup.step(dve.tensor_scalar(ssm_u[:], dec[:], 9.998, 9.998, ALU.mult, ALU.add))
            setup.step(dve.tensor_tensor(ssm_t[:], ssm_t[:], ssm_u[:], ALU.is_gt))
            setup.step(dve.tensor_tensor(ssm_u[:], dec[:], dec[:, :, 0:1].to_broadcast([P, NC, NS]), ALU.not_equal))
            setup.step(dve.tensor_tensor(ssm_t[:], ssm_t[:], ssm_u[:], ALU.add))
            setup.step(dve.scalar_tensor_tensor(out=w_eff[:], in0=wsum[:], scalar=-1.0, in1=wsum[:],
                                                op0=ALU.mult, op1=ALU.max))
            setup.step(dve.tensor_scalar(ssm_u[:], dec[:], 0.999, 0.999, ALU.mult, ALU.add))
            setup.step(dve.tensor_tensor(ssm_u[:, :, 0], w_eff[:], ssm_u[:, :, 0], ALU.is_gt))
            setup.step(dve.tensor_tensor(ssm_t[:, :, 0], ssm_t[:, :, 0], ssm_u[:, :, 0], ALU.add))
            setup.step(dve.tensor_reduce(viol[:], ssm_t[:].rearrange("p c d -> p (c d)"), AX_X, ALU.add))
            dve.wait_ge(s_bias_mm, 1)
            for k in range(KD):
                setup.step(dve.tensor_scalar(wi[:, k, :], wi[:, k, :], gin[:, k:k + 1], None, ALU.mult))
            setup.end()
            dve.wait_ge(s_ready, 1)
            dve.tensor_scalar(flag[:], m_viol, 1.0, None, ALU.min).then_inc(s_flag, 1)
            dve.wait_ge(s_flag, 1)
            dve.tensor_copy(general[:], flag[0:1, :]).then_inc(s_flag, 1)
            dve.tensor_scalar(w_eff[:], wsum[:], -1.0, 1.0, ALU.mult, ALU.add).then_inc(s_flag, 1)
            dve.wait_ge(s_flag, 3)
            dve.scalar_tensor_tensor(out=w_eff[:], in0=w_eff[:], scalar=flag[:, 0:1], in1=wsum[:],
                                     op0=ALU.mult, op1=ALU.add).then_inc(s_flag, 1)
            dve.wait_ge(s_flag, 4)
            for c in range(NC):
                dve.tensor_scalar(wo[:, c, :], wo[:, c, :], w_eff[:, c:c + 1], None, ALU.mult).then_inc(s_flag, 1)

            def scales(sem_sum, n, col, chain, k, inv, inv_log):
                dve.wait_ge(sem_sum, n + 1)
                dve.tensor_copy(square_sum[:], m_square).then_inc(chain, 1)
                dve.wait_ge(chain, k + 1)
                dve.tensor_scalar(half_exp[:], square_sum[:].bitcast(I32), 24, None,
                                  ALU.logical_shift_right).then_inc(chain, 1)
                dve.wait_ge(chain, k + 2)
                dve.tensor_scalar(inv, half_exp[:], float(1 << 23), float((50 - inv_log) << 23),
                                  ALU.mult, ALU.add).then_inc(chain, 1)
                return dve.tensor_scalar(w_scale[:, col:col + 1], half_exp[:], -float(1 << 23), float(204 << 23),
                                         ALU.mult, ALU.add)

            scales(s_wi_sum, 0, 0, s_wi_scale, 0, wi_inv[:], X_SCALE_LOG).then_inc(s_wi_scale, 1)
            dve.wait_ge(s_wi_scale, 4)
            dve.wait_ge(s_wi_h, 1)
            dve.scalar_tensor_tensor(out=wil[:], in0=wi, scalar=w_scale[:, 0:1].bitcast(F32), in1=wih[:],
                                     op0=ALU.mult, op1=ALU.subtract).then_inc(s_wi_l, 1)
            is_general = dve.value_load(general[0:1, 0:1], min_val=0, max_val=1 << 20)

            ch_a = Chain(dve, s_a_dve, 2 * CT)
            ch_b = Chain(dve, s_b_dve, 2)
            ch_c = Chain(dve, s_c_dve, 2 * CT)
            ch_r = Chain(dve, s_r_dve, 2 * CT)
            ch_d = Chain(dve, s_d_dve, 6 + 2 * CT)
            ch_s = Chain(dve, s_s_dve, 4)

            def norm_stats(ch, n, src):
                for c in range(CT):
                    ch.link(dve.bn_stats(stats[:, n, c, :], src[:, c, :]))
                ch.wait_apart(held, (s_const, 160))
                for c in range(CT):
                    ch.link(dve.bn_aggr(mv[:, n, c, :], stats[:, n, c, :]))
                ch.wait()

            def input_stats(at):
                b, par, half = at
                ch_a.begin(b)
                ch_a.wait()
                dve.wait_ge(s_x[par], 16 * (half + 1))
                if not first(b, 1):
                    dve.wait_ge(s_a_rstd, b)
                norm_stats(ch_a, 0, x_in[par])
                dve.tensor_scalar(var[:, 0, :], mv[:, 0, :, 1], (1.0 + LN_EPS) / X_SCALE ** 2,
                                  (LN_EPS / X_SCALE) ** 2, ALU.mult, ALU.add).then_inc(s_a_var, 1)
                ch_a.end()

            def general_scan(par):
                dve.memset(ssm_t[:], 0.0)
                dve.drain()
                with dve.Fori(0, L) as t:
                    dve.tensor_tensor(ssm_t[:], ssm_t[:], dec[:], ALU.mult)
                    dve.tensor_tensor(ssm_u[:], bmat[:], xs[par][:, :, bass.ds(t, 1)].to_broadcast([P, NC, NS]),
                                      ALU.mult)
                    dve.drain()
                    dve.scalar_tensor_tensor(out=ssm_t[:], in0=ssm_u[:], scalar=0.1, in1=ssm_t[:],
                                             op0=ALU.mult, op1=ALU.add)
                    dve.drain()
                    dve.tensor_scalar(ssm_t[:], ssm_t[:], CLIP, -CLIP, ALU.min, ALU.max)
                    dve.drain()
                    dve.tensor_tensor(ssm_u[:], ssm_t[:], cmat[:], ALU.mult)
                    dve.drain()
                    dve.tensor_reduce(state[:, :, bass.ds(t, 1)], ssm_u[:], AX_X, ALU.add)
                    dve.drain()
                dve.tensor_scalar(state[:], state[:], CLIP, -CLIP, ALU.min, ALU.max)

            def scan(at):
                b, par, half = at
                ch_b.begin(b)
                dve.wait_ge(s_projc, 2 * NC * (b + 1))
                if not first(b, 1):
                    dve.wait_ge(s_z, b)
                ch_b.link(dve.tensor_scalar(xs[par][:], xs[par][:], CLIP, -CLIP, ALU.min, ALU.max))
                ch_b.link(dve.tensor_scalar(gate[par][:], gate[par][:], TANH_CLIP, -TANH_CLIP, ALU.min, ALU.max))
                ch_b.wait_apart(held, (s_flag, 1))
                with dve.If(is_general != 0):
                    general_scan(par)
                with dve.Else():
                    dve.tensor_tensor_scan(state[:].rearrange("p c t -> p (c t)"),
                                           decay_row[:].rearrange("p c t -> p (c t)"),
                                           xs[par][:].rearrange("p c t -> p (c t)"), 0.0, ALU.mult, ALU.add)
                dve.drain()
                dve.tensor_tensor(gate[par][:], state[:], gate[par][:], ALU.mult).then_inc(s_z, 1)
                ch_b.end()

            def residual(at):
                b, par, half = at
                ch_r.begin(b)
                ch_r.wait()
                dve.wait_ge(s_gain, b + 1)
                dve.wait_ge(s_resb, b + 1)
                dve.tensor_tensor(x_res[par][:], o[:], x_res[par][:], ALU.add).then_inc(s_xnew, 1)
                dve.wait_ge(s_xnew, b + 1)
                if not first(b, 1):
                    dve.wait_ge(s_r_rstd, b)
                norm_stats(ch_r, 2, x_res[par])
                dve.tensor_scalar(var[:, 2, :], mv[:, 2, :, 1], 1.0 / X_SCALE ** 2, LN_EPS / X_SCALE ** 2,
                                  ALU.mult, ALU.add).then_inc(s_r_var, 1)
                ch_r.end()

            def w1_scale(e):
                if not first(e, 1):
                    dve.wait_ge(s_w1_l, e)
                    dve.wait_ge(s_w2_l, e)
                    dve.wait_ge(s_row_max, e)
                scales(s_w1_sum, e, 0, s_w1_chain, 3 * e, w1_inv[:, bass.ds(e, 1)],
                       X_SCALE_LOG).then_inc(s_w1_scale, 1)

            def w1_low(e):
                dve.wait_ge(s_w1_h, 2 * (e + 1))
                dve.wait_ge(s_w1_scale, e + 1)
                dve.scalar_tensor_tensor(out=w1_part(w1l, e), in0=stage[:], scalar=w_scale[:, 0:1].bitcast(F32),
                                         in1=w1_part(w1h, e), op0=ALU.mult, op1=ALU.subtract).then_inc(s_w1_l, 1)

            def y_bound(e):
                chain, k = s_row_chain, 4 * e
                dve.wait_ge(s_w1_scale, e + 1)
                dve.wait_ge(s_row_sq, e + 1)
                for h in range(2):
                    ins = dve.tensor_reduce(row_max[:, h:h + 1], PT[h][:, :], AX_X, ALU.max)
                ins.then_inc(chain, 1)
                dve.wait_ge(chain, k + 1)
                dve.tensor_tensor(row_max[:, 0:1], row_max[:, 0:1], row_max[:, 1:2], ALU.max).then_inc(chain, 1)
                dve.wait_ge(chain, k + 2)
                dve.tensor_scalar(row_exp[:], row_max[:, 0:1].bitcast(I32), 23, None,
                                  ALU.logical_shift_right).then_inc(chain, 1)
                dve.wait_ge(chain, k + 3)
                dve.tensor_scalar(y_exp[:, bass.ds(e, 1)], row_exp[:], float(1 << 23), -float(133 << 23),
                                  ALU.mult, ALU.add)
                dve.tensor_scalar(row_exp[:], row_exp[:], -float(1 << 23), float(133 << 23),
                                  ALU.mult, ALU.add).then_inc(chain, 1)
                dve.wait_ge(chain, k + 4)
                dve.scalar_tensor_tensor(out=up_scale[:, bass.ds(e, 1)], in0=row_exp[:], scalar=1.0,
                                         in1=w1_inv[:, bass.ds(e, 1)], op0=ALU.mult, op1=ALU.add).then_inc(s_row_max, 1)

            def w2_scale(e):
                dve.wait_ge(s_w1_l, e + 1)
                dve.wait_ge(s_row_max, e + 1)
                if not first(e, 1):
                    dve.wait_ge(s_w2_l, e)
                scales(s_w2_sum, e, 1, s_w2_chain, 4 * e, w2_inv[:], 0).then_inc(s_w2_scale, 1)
                dve.wait_ge(s_w2_chain, 4 * e + 3)
                dve.scalar_tensor_tensor(out=y_inv[:, bass.ds(e, 1)], in0=w2_inv[:], scalar=1.0,
                                         in1=y_exp[:, bass.ds(e, 1)], op0=ALU.mult,
                                         op1=ALU.add).then_inc(s_w2_chain, 1)
                dve.wait_ge(s_w2_chain, 4 * e + 4)
                dve.tensor_scalar(y_inv[:, bass.ds(e, 1)], y_inv[:, bass.ds(e, 1)], float(1 << 23), None,
                                  ALU.max).then_inc(s_y_inv, 1)

            def w2_low(e):
                dve.wait_ge(s_w2_h, 2 * (e + 1))
                dve.wait_ge(s_w2_scale, e + 1)
                dve.scalar_tensor_tensor(out=w2_part(w2l, e), in0=stage2[:], scalar=w_scale[:, 1:2].bitcast(F32),
                                         in1=w2_part(w2h, e), op0=ALU.mult, op1=ALU.subtract).then_inc(s_w2_l, 1)

            def logits_less_max(at):
                b, par, half = at
                ch = ch_d
                ch.begin(b)
                ch.wait()
                dve.wait_ge(s_logit, b + 1)
                ch.link(dve.tensor_reduce(mx[:], m_logit, AX_X, ALU.max))
                ch.wait()
                dve.tensor_tensor(lg[:], m_logit, mx[:].unsqueeze(2).to_broadcast([P, CT, E]),
                                  ALU.subtract).then_inc(s_lg, 1)

            def out_clip_and_choose(w, d):
                c_, d_ = ch_c, ch_d
                if w:
                    b = w[0]
                    c_.begin(b)
                    c_.wait()
                    if not first(b, 1):
                        dve.wait_ge(s_xnew, b)
                        dve.wait_ge(s_c_rstd, b)
                    for h in range(2):
                        dve.wait_ge(s_omm, CT * b + (h + 1) * CT // 2)
                        dve.tensor_scalar(o[:, 2 * h:2 * h + 2, :],
                                          PO[h][:, :].rearrange("p (c d) -> p c d", d=D), CLIP, -CLIP,
                                          ALU.min, ALU.max).then_inc(s_o, 1)
                if d:
                    if not first(d[0], 1):
                        dve.wait_ge(s_s_dve, 4 * d[0])
                    dve.wait_ge(s_ex, d[0] + 1)
                    d_.link(dve.tensor_reduce(den[:], ex[:], AX_X, ALU.add))
                if w:
                    dve.wait_ge(s_o, 2 * (w[0] + 1))
                    for c in range(CT // 2):
                        c_.link(dve.bn_stats(stats[:, 1, c, :], o[:, c, :]))
                if d:
                    d_.wait()
                    d_.link(dve.reciprocal(mx[:], den[:]))
                if w:
                    for c in range(CT // 2, CT):
                        c_.link(dve.bn_stats(stats[:, 1, c, :], o[:, c, :]))
                if d:
                    d_.wait()
                    d_.link(dve.tensor_tensor(prob[:], ex[:], mx[:].unsqueeze(2).to_broadcast([P, CT, E]), ALU.mult))
                if w:
                    c_.wait_apart(held, (s_const, 160))
                    for c in range(CT):
                        c_.link(dve.bn_aggr(mv[:, 1, c, :], stats[:, 1, c, :]))
                if d:
                    d_.wait_apart(held, (s_const, 160))
                    for c in range(CT):
                        d_.link(dve.max(top[:, c, :], prob[:, c, :]))
                if w:
                    c_.wait()
                    dve.tensor_scalar(var[:, 1, :], mv[:, 1, :, 1], LN_EPS, None, ALU.add).then_inc(s_c_var, 1)
                    c_.end()
                if d:
                    d_.wait_apart(held, (s_const, 160))
                    for c in range(CT):
                        d_.link(dve.max_index(top_i[:, c, :], top[:, c, :], prob[:, c, :]))
                    d_.wait()
                    d_.link(dve.tensor_copy(top_f[:], top_i[:, :, 0:TOP]))
                    d_.wait()
                    for k in range(TOP):
                        ins = dve.tensor_tensor(hot[:, k, :, :], iota8[:].unsqueeze(1).to_broadcast([P, CT, E]),
                                                top_f[:, :, k:k + 1].to_broadcast([P, CT, E]), ALU.is_equal)
                    d_.link(ins)
                    d_.wait()
                    dve.tensor_tensor(mask[:, 0:CT, :], hot[:, 0, :, :], hot[:, 1, :, :], ALU.add).then_inc(s_mask, 1)
                    d_.end()

            def place(at):
                b, par, half = at
                ch = ch_s
                ch.begin(b)
                ch.wait()
                dve.wait_ge(s_rank, b + 1)
                if not first(b, 1):
                    dve.wait_ge(s_rankread, b)
                ch.link(dve.tensor_tensor(slot_f[:], m_rank[:, 0:CT, :],
                                          cnt[:].unsqueeze(1).to_broadcast([P, CT, E]), ALU.add))
                ch.wait()
                dve.tensor_tensor(cnt[:], cnt[:], m_rank[:, CT, :], ALU.add).then_inc(s_rankread, 1)
                for k in range(TOP):
                    ins = dve.tensor_tensor(pick[:, k, :, :], hot[:, k, :, :], slot_f[:], ALU.mult)
                ch.link(ins)
                ch.wait()
                ch.link(dve.tensor_reduce(slot_sum[:], pick[:], AX_X, ALU.add))
                if not first(b, 2):
                    dve.wait_ge(s_rows[par], 16 * TOP * CT * half)
                ch.wait()
                dve.tensor_copy(slot[par][:], slot_sum[:])
                for k in range(TOP):
                    dve.tensor_copy(row[par][:, k, :, 0], ids[:])
                    ins = dve.tensor_copy(row[par][:, k, :, 1].bitcast(F32), top[:, :, k])
                ins.then_inc(s_slot, 1)
                ch.link(dve.tensor_scalar(ids[:], ids[:], float(L), None, ALU.add))
                ch.end()

            def step(m, u):
                at = [lagged(m, u, n, NB) for n in range(LAGS + 1)]
                if at[STATS]:
                    input_stats(at[STATS])
                if u == 0 and at[2]:
                    w1_low(m - 1)
                if u == 1 and at[3]:
                    w2_low(m - 1)
                if at[PLACE]:
                    place(at[PLACE])
                if at[SCAN]:
                    scan(at[SCAN])
                if at[STATS] and u == 1:
                    w1_scale(m)
                if at[W2] and u == 0:
                    w2_scale(m - 1)
                if at[RESIDUAL]:
                    residual(at[RESIDUAL])
                if at[ROUTE]:
                    logits_less_max(at[ROUTE])
                out_clip_and_choose(at[UNPROJECT], at[ROUTE])
                if at[STATS] and u == 1:
                    y_bound(m)

            batches(dve, step)

            dve.wait_ge(s_rankread, NB)
            n = 0

            def chained(ins):
                nonlocal n
                ins.then_inc(s_tile_tab, 1)
                n += 1
                dve.wait_ge(s_tile_tab, n)

            chained(dve.tensor_scalar(n_e[:], iota8[0:1, :], -float(REGION), None, ALU.mult))
            chained(dve.tensor_tensor(n_e[:], n_e[:], cnt[0:1, :], ALU.add))
            chained(dve.tensor_tensor(cmp_t, n_e[:].unsqueeze(2).to_broadcast([1, E, T // P]),
                                      step128[:].unsqueeze(1).to_broadcast([1, E, T // P]), ALU.is_gt))
            chained(dve.tensor_reduce(tiles_e[:], cmp_t, AX_X, ALU.add))
            chained(dve.tensor_tensor_scan(incl[:], ones8[:], tiles_e[:], 0.0, ALU.mult, ALU.add))
            chained(dve.tensor_tensor(past, tile_no[:].unsqueeze(2).to_broadcast([1, NT, E - 1]),
                                      incl[:, 0:E - 1].unsqueeze(1).to_broadcast([1, NT, E - 1]), ALU.is_ge))
            chained(dve.tensor_tensor(past_t, past,
                                      tiles_e[:, 0:E - 1].unsqueeze(1).to_broadcast([1, NT, E - 1]), ALU.mult))
            chained(dve.tensor_reduce(e_of[:], past, AX_X, ALU.add))
            chained(dve.tensor_reduce(start_of[:], past_t, AX_X, ALU.add))
            chained(dve.tensor_tensor(row_f[:], tile_no[:], start_of[:], ALU.subtract))
            chained(dve.tensor_scalar(row_f[:], row_f[:], float(P), None, ALU.mult))
            chained(dve.scalar_tensor_tensor(out=row_f[:], in0=e_of[:], scalar=float(REGION), in1=row_f[:],
                                             op0=ALU.mult, op1=ALU.add))
            dve.tensor_copy(tile_row[:], row_f[:]).then_inc(s_tiles, 1)
            dve.tensor_copy(tile_e[:], e_of[:]).then_inc(s_tiles, 1)

            def low_part(at):
                j, par, _, _, _ = at
                dve.wait_ge(s_gtc, j + 1)
                if not first(j, 2):
                    dve.wait_ge(s_h, j - 1)
                dve.tensor_tensor(xgl[par], PR[:, 0:D].rearrange("p (k q) -> p k q", k=KD), xgh[par],
                                  ALU.subtract).then_inc(s_xg_l, 1)

            def y_low(at):
                j, par, _, _, _ = at
                dve.wait_ge(s_ytc, j + 1)
                if not first(j, 2):
                    dve.wait_ge(s_mo, j - 1)
                dve.tensor_tensor(ytl[par], PO[1][:, :].rearrange("p (k q) -> p k q", k=KI), yth[par],
                                  ALU.subtract).then_inc(s_y_l, 1)

            def weighted(at, e):
                j, par, uses, i, tb_uses = at
                dve.wait_ge(s_mo, j + 1)
                if not first(j, 2):
                    dve.wait_ge(s_add[par], 16 * uses)
                dve.wait_ge(s_tb[i], 16 * (tb_uses + 1))
                dve.tensor_scalar(y_out[par], PO[0][:, 0:D], tb[i][:, 1:2].bitcast(F32),
                                  y_inv[:, bass.ds(e, 1)].bitcast(F32), ALU.mult, ALU.mult).then_inc(s_yout, 1)

            def tile_step(m, u):
                now, last, old, nxt = (tile(m, u, n) for n in (0, 1, 2, -1))
                e_now, e_old = (at and dve.value_load(tile_e[0:1, bass.ds(at[0], 1)], min_val=0, max_val=E - 1)
                                for at in (now, old))
                if nxt:
                    low_part(nxt)
                if last:
                    y_low(last)
                if now:
                    j, par, _, _, _ = now
                    dve.wait_ge(s_h, j + 1)
                    dve.wait_ge(s_silu, j + 1)
                    if not first(j, 2):
                        dve.wait_ge(s_yt, j - 1)
                    dve.scalar_tensor_tensor(out=act_y[par], in0=[PT, PG][par][1][:, :],
                                             scalar=up_scale[:, bass.ds(e_now, 1)].bitcast(F32), in1=act_s[par],
                                             op0=ALU.mult, op1=ALU.mult).then_inc(s_y, 1)
                if old:
                    weighted(old, e_old)

            dve.wait_ge(s_y_inv, E)
            dve.wait_ge(s_tiles, 2)
            low_part(tile(0, 0, 0))
            tiles(dve, tile_step, ahead=1)

        @block.tensor
        def _(pe):
            pe.wait_ge(s_const, 160)
            pe.wait_ge(s_pool0, 19)
            for j in range(2 * NC):
                for k in range(KD):
                    ins = pe.matmul(m_bias[:, j:j + 1], wi[:, k, j * P:(j + 1) * P], bin_[:, k:k + 1],
                                    start=(k == 0), stop=(k == KD - 1))
            ins.then_inc(s_bias_mm, 1)
            pe.wait_ge(s_setup, SETUP)
            pe.wait_ge(s_biascopy, 1)
            pe.matmul(m_viol, onesf[:], viol[:], start=True, stop=True).then_inc(s_ready, 1)
            pe.wait_ge(s_wi_sq, 1)
            pe.wait_ge(s_flag, 1)
            pe.matmul(m_square, onesf[:], squares[:, 0:1], start=True, stop=True).then_inc(s_wi_sum, 1)

            def three_passes(out_ap, high, low, w_high, w_low, chunks):
                n = 0
                for a, w in ((high, w_high), (low, w_high), (high, w_low)):
                    for k in range(chunks):
                        ins = pe.matmul(out_ap, a(k), w(k), start=(n == 0), stop=(n == 3 * chunks - 1))
                        n += 1
                return ins

            def step(m, u):
                at_w1, at_w2, at_a, at_w, at_d, at_s = (lagged(m, u, n, NB)
                                                        for n in (STATS, W2, PROJECT, UNPROJECT, ROUTE, PLACE))

                def unproject(h):
                    b, par, half = at_w
                    pe.wait_ge(s_z, b + 1)
                    if not first(b, 1):
                        pe.wait_ge(s_o, 2 * b)
                    for c in range(2 * h, 2 * h + 2):
                        for k in range(NC):
                            ins = pe.matmul(PO[h][:, (c % 2) * D:(c % 2 + 1) * D],
                                            gate[par][:, k, c * P:(c + 1) * P], wo[:, k, :],
                                            start=(k == 0), stop=(k == NC - 1))
                        ins.then_inc(s_omm, 1)

                def turn_r(k):
                    b = at_d[0]
                    if not first(b, 1) or k > 0:
                        pe.wait_ge(s_trc, KD * b + k)
                    for c in range(CT):
                        ins = pe.transpose(PR[:, c * P:(c + 1) * P], r[:, c, k * P:(k + 1) * P], ident[:])
                    ins.then_inc(s_tr, 1)

                def router():
                    b = at_d[0]
                    pe.wait_ge(s_trc, KD * (b + 1))
                    if not first(b, 1):
                        pe.wait_ge(s_rankread, b)
                    for c in range(CT):
                        for k in range(KD):
                            ins = pe.matmul(m_logit[:, c, :], r_t[:, k, c * P:(c + 1) * P], rw[:, k, :],
                                            start=(k == 0), stop=(k == KD - 1))
                    ins.then_inc(s_logit, 1)

                def ranks():
                    pe.wait_ge(s_mask, at_s[0] + 1)
                    pe.matmul(m_rank, upper[:], mask[:], start=True, stop=False, skip_group_check=True)
                    for c in range(CT):
                        ins = pe.matmul(m_rank[:, c + 1:, :], onesb[:],
                                        mask[:, c:c + 1, :].to_broadcast([P, CT - c, E]),
                                        start=False, stop=(c == CT - 1), skip_group_check=True)
                    ins.then_inc(s_rank, 1)

                if at_w:
                    unproject(0)
                if at_a:
                    b, par, half = at_a
                    pe.wait_ge(s_xhat, CT * (b + 1))
                    if not first(b, 1):
                        pe.wait_ge(s_txc, 2 * KD * b)
                    if first(b, 1):
                        pe.wait_ge(s_wi_scale, 4)
                    if u == 0:
                        pe.wait_ge(s_row_max, m)
                    elif not first(m, 1):
                        pe.wait_ge(s_w2_scale, m)
                    for k in range(KD):
                        for c in range(CT):
                            ins = pe.matmul(PT[k][:, c * P:(c + 1) * P], xhat[:, c, k * P:(k + 1) * P], ident[:],
                                            is_transpose=True, start=(c == 0), stop=False, skip_group_check=True)
                        ins.then_inc(s_tx, 1)
                if at_s:
                    ranks()
                if at_d:
                    pe.wait_ge(s_r, CT * (at_d[0] + 1))
                    turn_r(0)
                if at_a:
                    for k in range(KD):
                        pe.wait_ge(s_txc, 2 * KD * b + k + 1)
                        pe.matmul(PT[k][:, :], minus_id[:], xh_t[:, k, :], start=False, stop=True,
                                  skip_group_check=True).then_inc(s_low, 1)
                if at_w:
                    unproject(1)
                if at_d:
                    turn_r(1)
                if at_a:
                    pe.wait_ge(s_txc, 2 * KD * (b + 1))
                if at_w1 and u == 1:
                    pe.wait_ge(s_w1_sq, m + 1)
                    pe.matmul(m_square, onesf[:], squares[:, 0:1], start=True, stop=True).then_inc(s_w1_sum, 1)
                if at_w2 and u == 0:
                    pe.wait_ge(s_w2_sq, m)
                    pe.matmul(m_square, onesf[:], squares[:, 1:2], start=True, stop=True).then_inc(s_w2_sum, 1)
                if at_a:
                    if first(b, 1):
                        pe.wait_ge(s_wi_l, 1)
                    for j in range(2 * NC):
                        if at_d and j == 1:
                            router()
                        if not (first(b, 1) and j < 2):
                            pe.wait_ge(s_projc, 2 * NC * b + j - 1)
                        cols = slice(j * P, (j + 1) * P)
                        three_passes(PG[j % 2][:, :], lambda k: wih[:, k, cols], lambda k: wil[:, k, cols],
                                     lambda k: xh_t[:, k, :], lambda k: xl_t[:, k, :], KD).then_inc(s_proj, 1)
                elif at_d:
                    router()
                if at_w1 and u == 1:
                    pe.wait_ge(s_w1_scale, m + 1)
                    for h in range(2):
                        for k in range(KD):
                            ins = pe.matmul(PT[h][:, :], onesb[:],
                                            w1l[:, k, bass.ds(m * I2 + h * I, I)].bitcast(BF16),
                                            start=(k == 0), stop=(k == KD - 1))
                    ins.then_inc(s_row_sq, 1)

            batches(pe, step)
            pe.wait_ge(s_w1_l, E)
            pe.wait_ge(s_w2_l, E)
            pe.wait_ge(s_tiles, 2)
            pe.wait_ge(s_rankread, NB)
            pe.wait_ge(s_projc, 2 * NC * NB)

            def gathered(at):
                j, par, uses, _, _ = at
                pe.wait_ge(s_xg[par], 16 * (uses + 1))
                if not first(j, 1):
                    pe.wait_ge(s_xg_l, j)
                for k in range(KD):
                    ins = pe.transpose(PR[:, k * P:(k + 1) * P], xg[par][:, k * P:(k + 1) * P], ident[:])
                ins.then_inc(s_gt, 1)

            def hidden(at, e, h):
                j, par, _, _, _ = at
                if h == 0:
                    pe.wait_ge(s_gtc, j + 1)
                    pe.wait_ge(s_xg_l, j + 1)
                    if not first(j, 2):
                        pe.wait_ge(s_y, j - 1)
                cols = bass.ds(e * I2 + h * I, I)
                three_passes([PT, PG][par][h][:, :], lambda k: xgh[par][:, k, :],
                             lambda k: xgl[par][:, k, :], lambda k: w1h[:, k, cols],
                             lambda k: w1l[:, k, cols], KD).then_inc([s_hg, s_h][h], 1)

            def turned(at):
                j, par, _, _, _ = at
                pe.wait_ge(s_y, j + 1)
                if not first(j, 1):
                    pe.wait_ge(s_y_l, j)
                for k in range(KI):
                    ins = pe.transpose(PO[1][:, k * P:(k + 1) * P], act_y[par][:, k * P:(k + 1) * P], ident[:])
                ins.then_inc(s_yt, 1)

            def combined(at, e):
                j, par, _, _, _ = at
                pe.wait_ge(s_ytc, j + 1)
                pe.wait_ge(s_y_l, j + 1)
                if not first(j, 1):
                    pe.wait_ge(s_yout, j)
                three_passes(PO[0][:, 0:D], lambda k: yth[par][:, k, :], lambda k: ytl[par][:, k, :],
                             lambda k: w2_part(w2h, e)[:, k, :], lambda k: w2_part(w2l, e)[:, k, :],
                             KI).then_inc(s_mo, 1)

            def tile_step(m, u):
                now, last, old, nxt = (tile(m, u, n) for n in (0, 1, 2, -1))
                e_now, e_old = (at and pe.value_load(tile_e[0:1, bass.ds(at[0], 1)], min_val=0, max_val=E - 1)
                                for at in (now, old))
                if now:
                    hidden(now, e_now, 0)
                if nxt:
                    gathered(nxt)
                if last:
                    turned(last)
                if now:
                    hidden(now, e_now, 1)
                if old:
                    combined(old, e_old)

            gathered(tile(0, 0, 0))
            tiles(pe, tile_step, ahead=1)


def kernel(L0_attn_x, L0_attn_W_in, L0_attn_W_out, L0_attn_A_log, L0_attn_B, L0_attn_C, L0_attn_ln_in_g,
           L0_attn_ln_in_b, L0_attn_ln_out_g, L0_attn_ln_out_b, L0_ffn_w1, L0_ffn_w2, L0_ffn_router_w):
    import numpy as np
    import concourse.bacc as bacc
    from concourse.bass_utils import run_bass_kernel_spmd

    given = {
        "x": L0_attn_x,
        "w_in_t": np.transpose(L0_attn_W_in),
        "w_out_t": np.transpose(L0_attn_W_out),
        "a_log": L0_attn_A_log,
        "b_in": L0_attn_B,
        "c_out": L0_attn_C,
        "g_in": np.transpose(L0_attn_ln_in_g.reshape(-1, P)),
        "bias_in": np.transpose(L0_attn_ln_in_b.reshape(-1, P)),
        "g_out": L0_attn_ln_out_g,
        "bias_out": L0_attn_ln_out_b,
        "w1_t": np.transpose(L0_ffn_w1, (0, 2, 1)),
        "w2_t": np.transpose(L0_ffn_w2, (0, 2, 1)),
        "router_t": np.transpose(L0_ffn_router_w),
    }
    nc = bacc.Bacc("TRN2", target_bir_lowering=False, num_devices=1)
    arrays, args = {}, {}
    for name, a in given.items():
        arrays[name] = np.ascontiguousarray(a)
        args[name] = nc.dram_tensor(name, a.shape, mybir.dt.from_np(arrays[name].dtype), kind="ExternalInput").ap()
    out = nc.dram_tensor("out", L0_attn_x.shape, F32, kind="ExternalOutput").ap()
    build(nc, **args, out=out)
    got = run_bass_kernel_spmd(nc, [arrays], core_ids=[0])
    return got.results[0]["out"]
```
